# Optimizing a Trainium2 kernel written in Bass

```python
import numpy as np
import jax
import jax.numpy as jnp

def _softmax(x, axis=-1):
    return jax.nn.softmax(x, axis=axis)
def _gelu(x):
    return jax.nn.gelu(x, approximate=True)
def _silu(x):
    return jax.nn.silu(x)
def _sigmoid(x):
    return jax.nn.sigmoid(x)
def _layernorm(x, axis=-1, eps=1e-5):
    m = jnp.mean(x, axis=axis, keepdims=True)
    v = jnp.var(x, axis=axis, keepdims=True)
    return (x - m) / jnp.sqrt(v + eps)
def _scatter_add(tgt, idx, src, axis=0):
    return tgt.at[idx].add(src)
def _segment_sum(src, seg, n):
    return jax.ops.segment_sum(src, seg, n)

kernel_name = 'mk_adj_preln_d2_adj_512_f18b28'

def setup_inputs(seed: int = 0):
    np.random.seed(seed)
    _w = jnp.asarray
    def _rec_inputs():
        import jax
        import jax.numpy as jnp
        _gk = jax.random.key(seed)
        x = -0.0002928 + 1 * jax.random.normal(jax.random.fold_in(_gk, 1), (64, 256, 512), jnp.float32)
        _a = jax.random.bernoulli(jax.random.fold_in(_gk, 2), 0.0625, (64, 256, 256))
        _a = jnp.logical_or(_a, jnp.swapaxes(_a, -1, -2))
        _a = jnp.logical_or(_a, jnp.eye(256, dtype=bool))
        adj = _a
        return x, adj
    x, adj = _rec_inputs()
    def _L0_gnn_setup():
        import jax, jax.numpy as jnp
        import numpy as np
        QUERY_DIM = 512
        HEADS = 4
        DIM_HEAD = 64
        INNER = HEADS * DIM_HEAD
        B, N = (4, 2048)
        key = jax.random.key(seed)
        ks = jax.random.split(key, 6)
        s = 1.0 / np.sqrt(QUERY_DIM)
        x = jax.random.normal(ks[0], (B, N, QUERY_DIM), dtype=jnp.float32)
        adjacency_mask = jax.random.randint(ks[1], (B, N, N), 0, 2) > 0
        Wq = jax.random.normal(ks[2], (QUERY_DIM, INNER), dtype=jnp.float32) * s
        Wk = jax.random.normal(ks[3], (QUERY_DIM, INNER), dtype=jnp.float32) * s
        Wv = jax.random.normal(ks[4], (QUERY_DIM, INNER), dtype=jnp.float32) * s
        Wo = jax.random.normal(ks[5], (INNER, QUERY_DIM), dtype=jnp.float32) * (1.0 / np.sqrt(INNER))
        bo = jnp.zeros((QUERY_DIM,), dtype=jnp.float32)
        return {'x': x, 'adjacency_mask': adjacency_mask, 'Wq': Wq, 'Wk': Wk, 'Wv': Wv, 'Wo': Wo, 'bo': bo}
    _L0_gnn_all = _L0_gnn_setup()
    _L0_gnn_in = {k: v for k, v in _L0_gnn_all.items() if k in ('Wq', 'Wk', 'Wv', 'Wo', 'bo', )}
    del _L0_gnn_all

    def _L1_gnn_setup():
        import jax, jax.numpy as jnp
        import numpy as np
        HEAD_NUM = 8
        THRESHOLD = 0.1
        NEG = -10000000000.0
        COS_EPS = 1e-08
        B, S, D = (8, 1024, 512)
        D_OUT = 512
        key = jax.random.key(seed)
        ks = jax.random.split(key, 12)
        embs = jax.random.normal(ks[0], (B, S, D), dtype=jnp.float32)
        lengths = jax.random.randint(ks[1], (B,), S // 2, S + 1)
        pad = jnp.arange(S)[None, :] >= lengths[:, None]
        score_mask = pad[:, :, None] | pad[:, None, :]
        sc = 1.0 / np.sqrt(D)
        mk = lambda k, shp: jax.random.normal(k, shp, dtype=jnp.float32) * sc
        return {'embs': embs, 'score_mask': score_mask, 'map_w': mk(ks[2], (D, D)), 'map_b': jnp.zeros((D,), jnp.float32), 'q_w': mk(ks[3], (D, D)), 'q_b': jnp.zeros((D,), jnp.float32), 'k_w': mk(ks[4], (D, D)), 'k_b': jnp.zeros((D,), jnp.float32), 'gcn_map_w': mk(ks[5], (D_OUT, D)), 'gcn_map_b': jnp.zeros((D_OUT,), jnp.float32), 'gcn_W': jax.random.normal(ks[6], (D_OUT // HEAD_NUM, D_OUT // HEAD_NUM), dtype=jnp.float32) * (1.0 / np.sqrt(D_OUT // HEAD_NUM))}
    _L1_gnn_all = _L1_gnn_setup()
    _L1_gnn_in = {k: v for k, v in _L1_gnn_all.items() if k in ('map_w', 'map_b', 'q_w', 'q_b', 'k_w', 'k_b', 'gcn_map_w', 'gcn_map_b', 'gcn_W', )}
    del _L1_gnn_all

    return {
        "x": x,
        "adj": adj,
        "L0_gnn_Wq": _L0_gnn_in["Wq"],
        "L0_gnn_Wk": _L0_gnn_in["Wk"],
        "L0_gnn_Wv": _L0_gnn_in["Wv"],
        "L0_gnn_Wo": _L0_gnn_in["Wo"],
        "L0_gnn_bo": _L0_gnn_in["bo"],
        "L1_gnn_map_w": _L1_gnn_in["map_w"],
        "L1_gnn_map_b": _L1_gnn_in["map_b"],
        "L1_gnn_q_w": _L1_gnn_in["q_w"],
        "L1_gnn_q_b": _L1_gnn_in["q_b"],
        "L1_gnn_k_w": _L1_gnn_in["k_w"],
        "L1_gnn_k_b": _L1_gnn_in["k_b"],
        "L1_gnn_gcn_map_w": _L1_gnn_in["gcn_map_w"],
        "L1_gnn_gcn_map_b": _L1_gnn_in["gcn_map_b"],
        "L1_gnn_gcn_W": _L1_gnn_in["gcn_W"],
    }

def reference(x, adj, L0_gnn_Wq, L0_gnn_Wk, L0_gnn_Wv, L0_gnn_Wo, L0_gnn_bo, L1_gnn_map_w, L1_gnn_map_b, L1_gnn_q_w, L1_gnn_q_b, L1_gnn_k_w, L1_gnn_k_b, L1_gnn_gcn_map_w, L1_gnn_gcn_map_b, L1_gnn_gcn_W):
    import jax
    import jax.numpy as jnp
    def _L0_gnn_ref(x, adjacency_mask, Wq, Wk, Wv, Wo, bo):
        import jax, jax.numpy as jnp
        import numpy as np
        QUERY_DIM = 512
        HEADS = 4
        DIM_HEAD = 64
        INNER = HEADS * DIM_HEAD
        B, N = (4, 2048)
        scale = DIM_HEAD ** (-0.5)

        def split_heads(t):
            b, n, _ = t.shape
            return t.reshape(b, n, HEADS, DIM_HEAD).transpose(0, 2, 1, 3)
        q = split_heads(x @ Wq)
        k = split_heads(x @ Wk)
        v = split_heads(x @ Wv)
        sim = jnp.einsum('bhid,bhjd->bhij', q, k) * scale
        neg = -jnp.finfo(sim.dtype).max
        sim = jnp.where(adjacency_mask[:, None, :, :], sim, neg)
        attn = jax.nn.softmax(sim, axis=-1)
        out = jnp.einsum('bhij,bhjd->bhid', attn, v)
        out = out.transpose(0, 2, 1, 3).reshape(x.shape[0], x.shape[1], INNER)
        return out @ Wo + bo

    def _L1_gnn_ref(embs, score_mask, map_w, map_b, q_w, q_b, k_w, k_b, gcn_map_w, gcn_map_b, gcn_W):
        import jax, jax.numpy as jnp
        import numpy as np
        HEAD_NUM = 8
        THRESHOLD = 0.1
        NEG = -10000000000.0
        COS_EPS = 1e-08
        B, S, D = (8, 1024, 512)
        D_OUT = 512
        b, s, d = embs.shape
        h, dk = (HEAD_NUM, d // HEAD_NUM)
        sm = score_mask[:, None, :, :]
        keep = (~sm[..., 0:1]).astype(embs.dtype)
        m = embs @ map_w.T + map_b
        sem = m.reshape(b, s, h, dk).transpose(0, 2, 1, 3)
        norm = jnp.maximum(jnp.linalg.norm(sem, axis=-1, keepdims=True), COS_EPS)
        n = sem / norm
        cos = jnp.einsum('bhsd,bhtd->bhst', n, n)
        cos = cos * (~sm).astype(cos.dtype)
        cos_adj = (cos > THRESHOLD).astype(embs.dtype)
        q = (m @ q_w.T + q_b).reshape(b, s, h, dk).transpose(0, 2, 1, 3)
        k = (m @ k_w.T + k_b).reshape(b, s, h, dk).transpose(0, 2, 1, 3)
        scores = jnp.einsum('bhsd,bhtd->bhst', q, k) / jnp.sqrt(jnp.asarray(dk, embs.dtype))
        scores = jnp.where(sm, NEG, scores)
        p_attn = jax.nn.softmax(scores, axis=-1) * keep
        adj = cos_adj * p_attn
        hk = gcn_map_w.shape[0] // h
        sem_h = (embs @ gcn_map_w.T + gcn_map_b).reshape(b, s, h, hk).transpose(2, 0, 1, 3)
        adj_h = adj.transpose(1, 0, 2, 3)
        Ax = jnp.einsum('hbst,hbtd->hbsd', adj_h, sem_h)
        AxW = Ax @ gcn_W.T
        denom = adj_h.sum(-1, keepdims=True) + 1.0
        out = jax.nn.relu(AxW / denom)
        out = out.transpose(1, 2, 0, 3).reshape(b, s, h * hk)
        return out

    h = jnp.maximum(_layernorm(x, axis=-1), 0.0)
    x = x + _L0_gnn_ref(h, adj, L0_gnn_Wq, L0_gnn_Wk, L0_gnn_Wv, L0_gnn_Wo, L0_gnn_bo)
    h = jnp.maximum(_layernorm(x, axis=-1), 0.0)
    x = x + _L1_gnn_ref(h, adj, L1_gnn_map_w, L1_gnn_map_b, L1_gnn_q_w, L1_gnn_q_b, L1_gnn_k_w, L1_gnn_k_b, L1_gnn_gcn_map_w, L1_gnn_gcn_map_b, L1_gnn_gcn_W)
    return x


_drawn_inputs = setup_inputs


def setup_inputs(seed=0):
    import zlib

    import numpy as np

    out = dict(_drawn_inputs(seed))
    spreads = {'L0_gnn_bo': (0.0, 0.1),
     'L1_gnn_map_b': (0.0, 0.8),
     'L1_gnn_q_b': (0.0, 0.8),
     'L1_gnn_k_b': (0.0, 0.8),
     'L1_gnn_gcn_map_b': (0.0, 0.296)}
    factors = {'L1_gnn_map_w': 8.0, 'L1_gnn_q_w': 8.0, 'L1_gnn_k_w': 8.0}
    for name, (base, spread) in spreads.items():
        noise = np.random.default_rng([zlib.crc32(name.encode()), seed]).standard_normal(out[name].shape)
        drawn = base * np.exp(spread * noise) if base else spread * noise
        out[name] = jnp.asarray(drawn.astype(out[name].dtype))
    for name, factor in factors.items():
        out[name] = (out[name] * factor).astype(out[name].dtype)
    return out
```

```python
from contextlib import ExitStack

import numpy as np
import concourse.bass as bass
from concourse import mybir

F32 = mybir.dt.float32
F32R = mybir.dt.float32r
U8 = mybir.dt.uint8
ALU = mybir.AluOpType
ACT = mybir.ActivationFunctionType

PASSES = ((0, 0), (0, 1), (1, 0))
LN_EPS = 1e-5
COS_EPS = 1e-8
COS_THRESHOLD = 0.1
MASKED_L1 = -1e10
FLT_MAX = float(np.finfo(np.float32).max)


def gnn_two_layers(nc, x, adj, wq, wk, wv, wo, bo, map_t, map_b, q_t, q_b, k_t, k_b, gcn_map, gcn_map_b, gcn_t, out):
    G, N, D = x.shape
    C = N // 128
    KT = D // 128
    DH = 64
    INNER = wq.shape[1]
    H0, H1 = INNER // DH, D // DH
    PAIRS0, PAIRS1 = H0 // 2, H1 // 2
    SCALE = DH ** -0.5
    assert (C, KT, H0, H1) == (2, 4, 4, 8)

    ORDER = ["ht0a", "ht0b", ("score", 0), "qk0", "qk1", "v0", "s0", "exp0", "s1", ("exp", 0), ("cos", 0), "s2",
             "exp1", "sum0", "exp2", "s3", ("score", 1), "sum1", ("turn", 0), "exp3", "sum2", ("exp", 1),
             ("factor", 0), ("cos", 1), ("value", 0), "pt0", "sum3", "pt1", ("back", 0), ("factor", 1), "pt2",
             ("turn", 1), "pt3", ("score", 2), "av", ("value", 1), ("exp", 2), ("back", 1), "wo0", ("cos", 2), "wo1",
             ("turn", 2), ("score", 3), ("value", 2), ("factor", 2), "relu1", ("exp", 3), "ht1a", "ht1b", ("cos", 3),
             ("back", 2), "m0", ("turn", 3), "m1", ("value", 3), "m2", "vv0", ("factor", 3), "stats0", "rstd0", "m3",
             "vv1", "q0", "k0", "ss", ("back", 3), "q1", "relu0", "q2", "k1", "q3", "rt", "k2", "bc0", "bc1", "k3"]
    PRODUCTS = [s for s in ORDER if isinstance(s, str) and s[:3] not in ("exp", "sum", "sta", "rst", "rel")]
    SHORT = {"ss": 0, "rt": 1, "bc0": 2, "bc1": 3}
    LONG = [s for s in PRODUCTS if s not in SHORT]
    assert len(LONG) % 2 == 0
    bank_of = SHORT | {s: 6 + k % 2 for k, s in enumerate(LONG)}
    BY_VECTOR = [s for s in PRODUCTS if s[:2] != "pt"]
    HIGHS = [s for s in PRODUCTS if s[:2] in ("ht", "qk", "av") or (s[0] in "mqk" and s[1].isdigit())]

    def in_psum(n, name):
        return len(PRODUCTS) * n + PRODUCTS.index(name) + 1

    def out_of_psum(n, name):
        return len(BY_VECTOR) * (n + 1) + BY_VECTOR.index(name) + 1

    def room(n, name):
        k = LONG.index(name) - 2
        return out_of_psum(n, LONG[k]) - (0 if k >= 0 else len(BY_VECTOR))

    def pairs(a, p, steps=1):
        return steps * PAIRS1 * (a + 1) + steps * p

    ctx = ExitStack()
    with ctx:
        def sb(name, shape, dt=F32):
            return ctx.enter_context(nc.sbuf_tensor(name, shape, dt))

        w_qkv = sb("w_qkv", [128, 2, 3, KT, INNER], F32R)
        w_o = sb("w_o", [128, 2, PAIRS0, D], F32R)
        w_map = sb("w_map", [128, 2, KT, D], F32R)
        w_q = sb("w_q", [128, 2, KT, D], F32R)
        w_k = sb("w_k", [128, 2, KT, D], F32R)
        w_v = sb("w_v", [128, 2, KT, D], F32R)
        bias_o = sb("bias_o", [128, D])
        bias_v = sb("bias_v", [128, D])
        bias_m = sb("bias_m", [128, KT])
        bias_q = sb("bias_q", [128, KT])
        bias_k = sb("bias_k", [128, KT])
        ident = sb("ident", [128, 128])
        half_of = sb("half_of", [128, 2])
        pick = sb("pick", [40, PAIRS1, 128], F32R)
        minus_half = sb("minus_half", [128, 16])
        gcn_w = sb("gcn_w", [64, DH])
        gcn_b = sb("gcn_b", [64, H1])

        x_in = sb("x_in", [128, C, D])
        x_mid = sb("x_mid", [128, C, D])
        x_res = sb("x_res", [128, C, D])
        h = sb("h", [128, C, D])
        hT = sb("hT", [128, 2, KT, N], F32R)
        qkm = sb("qkm", [128, 2, KT, N], F32R)
        v0 = sb("v0", [128, C, INNER])
        prob0 = sb("prob0", [128, H0, C, N])
        ptm = sb("ptm", [128, H0, C * N])
        m32 = ptm[:, 0:2, :].rearrange("p a (b n) -> p (a b) n", n=N)
        msq = ptm[:, 2:4, :].rearrange("p a (b n) -> p (a b) n", n=N)
        oT0 = sb("oT0", [128, 2, PAIRS0, N], F32R)
        nrm = sb("nrm", [128, 2, KT, N], F32R)
        q1 = sb("q1", [128, 2, KT, N], F32R)
        k1 = sb("k1", [128, 2, KT, N], F32R)
        v1 = sb("v1", [128, C, D])
        att = sb("att", [128, 2, 2, C, N])
        uT = sb("uT", [128, 2, C * N])
        oT1 = sb("oT1", [128, N])
        pick_f = uT[0:40, 0, :].rearrange("p (t m) -> p t m", m=128)
        gcn_bb = v1[0:64, :, :].rearrange("p c (h m) -> p (c h) m", m=128)
        rel = sb("rel", [128, C, 128])
        adj8 = sb("adj8", [128, C, N], U8)
        mask0 = sb("mask0", [128, C, N])
        mask1 = sb("mask1", [128, C, N])
        keep = sb("keep", [128, C, 2])

        stats = sb("stats", [128, C, 6])
        mv = sb("mv", [128, C, 2])
        var_e = sb("var_e", [128, C])
        rstd = sb("rstd", [128, C])
        mr = sb("mr", [128, C])
        shift = sb("shift", [128, C])
        nmax0 = sb("nmax0", [128, H0, C])
        esum0 = sb("esum0", [128, H0, C])
        rsum0 = sb("rsum0", [128, H0, C])
        nmax1 = sb("nmax1", [128, PAIRS1, C, 2])
        esum1 = sb("esum1", [128, PAIRS1, C, 2])
        usum1 = sb("usum1", [128, PAIRS1, C, 2])
        den1 = sb("den1", [128, C, 2])
        rec1 = sb("rec1", [128, C, 2])
        fac1 = sb("fac1", [128, C, 2])
        ssq = sb("ssq", [128, C * H1])
        rn = sb("rn", [128, C * H1])
        rnT = sb("rnT", [40, N], F32R)

        bank = [ctx.enter_context(nc.psum_tensor(f"bank{b}", [128, 512], F32)) for b in range(8)]
        score_bank, gram_bank, t_bank = bank[0:2], bank[2:4], bank[4:6]

        def count(name):
            return ctx.enter_context(nc.semaphore(name))

        passed_sync, passed_gpsimd, passed_vector = count("passed_sync"), count("passed_gpsimd"), count("passed_vector")
        stage_in = [count(f"stage_in{k}") for k in range(4)]
        stage_hi = count("stage_hi")
        stage_lo = count("stage_lo")
        small_in = count("small_in")
        gcn_in = count("gcn_in")
        made = count("made")
        pick_made = count("pick_made")
        fold_full = count("fold_full")
        fold_hi = count("fold_hi")
        fold_done = count("fold_done")
        x_loaded = count("x_loaded")
        adj_loaded = count("adj_loaded")
        res_moved = count("res_moved")
        stored = count("stored")
        turn_full = count("turn_full")
        turn_done = count("turn_done")
        high_done = count("high_done")
        pT_ready = count("pT_ready")
        stat_done = count("stat_done")
        var_done = count("var_done")
        h_ready = count("h_ready")
        mask0_ready = count("mask0_ready")
        mid_ready = count("mid_ready")
        exp0_done = count("exp0_done")
        rsum0_done = count("rsum0_done")
        norm0_done = count("norm0_done")
        msq_done = count("msq_done")
        rn_done = count("rn_done")
        rt_high = count("rt_high")
        nhigh_done = count("nhigh_done")
        nlow_done = count("nlow_done")
        mask1_ready = count("mask1_ready")
        keep_ready = count("keep_ready")
        score_full = count("score_full")
        masked = count("masked")
        exp1_done = count("exp1_done")
        gram_full = count("gram_full")
        gated = count("gated")
        t_full = count("t_full")
        uT_ready = count("uT_ready")
        uv_full = count("uv_full")
        oT1_ready = count("oT1_ready")
        o_full = count("o_full")
        fac_steps = count("fac_steps")
        rel_done = count("rel_done")
        res_added = count("res_added")

        def rounds(eng, body):
            body(None, 0, True)
            with nc.Fori(0, G - 2, engines=[eng.engine], hint_back_edge=True) as a:
                body(a, a + 1, True)
            body(G - 2, G - 1, False)
            body(G - 1, None, False)

        def steps(a, n, more):
            return [s for s in ORDER if (isinstance(s, tuple) and a is not None)
                    or (isinstance(s, str) and n is not None and (more or s not in ("stats0", "rstd0", "relu0")))]

        def halves(w, dst):
            v = w.rearrange("(k p) n -> p k n", p=128)
            return [(v[:, 2 * i:2 * i + 2, :], [dst[:, s, 2 * i:2 * i + 2, :] for s in range(2)]) for i in range(KT // 2)]

        PIECES = [(w.rearrange("(k p) n -> p k n", p=128), [w_qkv[:, s, i, :, :] for s in range(2)])
                  for i, w in enumerate((wq, wk, wv))]
        PIECES += [(wo.rearrange("(k p) n -> p k n", p=128), [w_o[:, s, :, :] for s in range(2)])]
        PIECES += halves(map_t, w_map) + halves(q_t, w_q) + halves(k_t, w_k)
        slots = [att[:, 0, :, :, :], att[:, 1, :, :, :]]
        stage = [s.rearrange("p a b n -> p (a b n)") for s in slots]
        stage += [x_mid[:, :, :].rearrange("p a n -> p (a n)"), x_res[:, :, :].rearrange("p a n -> p (a n)")]
        gcn_rows = [prob0[0:64, :, :, :].rearrange("p a b n -> p (a b n)"), ptm[0:64, :, :].rearrange("p a n -> p (a n)")]

        def flat(ap):
            return ap.rearrange("p a b -> p (a b)")

        block = ctx.enter_context(nc.Block())

        @block.sync
        def _(sp):
            with nc.allow_non_contiguous_dma("small biases, once"):
                sp.dma_start(x_in[:, :, :], x[0].rearrange("(c p) d -> p c d", p=128)).then_inc(x_loaded, 16)
                sp.dma_start(adj8[:, :, :], adj[0].rearrange("(c p) j -> p c j", p=128)).then_inc(adj_loaded, 16)
                for k, (src, _) in enumerate(PIECES):
                    if k >= 4:
                        sp.wait_ge(stage_lo, k - 3)
                        sp.sem_inc(passed_sync, 1)
                    dst = stage[k % 4].rearrange("p (a n) -> p a n", n=src.shape[2])
                    sp.dma_start(dst, src).then_inc(stage_in[k % 4], 16)

            def body(a, n, more):
                if more:
                    sp.wait_ge(h_ready, 4 * n + 2)
                    sp.sem_inc(passed_sync, 1)
                    sp.wait_ge(mid_ready, 2 * n + 2)
                    sp.sem_inc(passed_sync, 1)
                    sp.dma_start(x_in[:, :, :], x[n + 1].rearrange("(c p) d -> p c d", p=128)).then_inc(x_loaded, 16)
                if a is not None:
                    sp.wait_ge(res_added, pairs(a, PAIRS1))
                    sp.sem_inc(passed_sync, 1)
                    sp.dma_start(out[a].rearrange("(c p) d -> p c d", p=128), x_res[:, :, :]).then_inc(stored, 16)
                if n is not None:
                    sp.wait_ge(turn_done, out_of_psum(n, "wo1"))
                    sp.sem_inc(passed_sync, 1)
                    if a is not None:
                        sp.wait_ge(stored, 16 * a + 16)
                        sp.sem_inc(passed_sync, 1)
                    sp.dma_start(x_res[:, :, :], x_mid[:, :, :]).then_inc(res_moved, 16)
                    if more:
                        sp.wait_ge(keep_ready, n + 1)
                        sp.sem_inc(passed_sync, 1)
                        sp.dma_start(adj8[:, :, :], adj[n + 1].rearrange("(c p) j -> p c j", p=128)).then_inc(adj_loaded, 16)

            rounds(sp, body)
            sp.wait_ge(stored, 16 * G)
            sp.sem_inc(passed_sync, 1)

        @block.gpsimd
        def _(pool):
            g = nc.gpsimd
            with nc.allow_non_contiguous_dma("small biases, once"):
                g.dma_start(bias_o[:, :], bo.partition_broadcast(128)).then_inc(small_in, 16)
                for dst, src in ((bias_m, map_b), (bias_q, q_b), (bias_k, k_b)):
                    g.dma_start(dst[:, :], src.rearrange("(k p) -> p k", p=128)).then_inc(small_in, 16)
                for half in range(2):
                    g.dma_start(gcn_rows[half].rearrange("p (h d) -> p h d", d=D),
                                gcn_map.rearrange("(h p) d -> p h d", p=DH)[:, 4 * half:4 * half + 4, :]).then_inc(gcn_in, 16)
                g.dma_start(gcn_w[:, :], gcn_t).then_inc(gcn_in, 16)
                g.dma_start(gcn_b[:, :], gcn_map_b.rearrange("(h p) -> p h", p=DH)).then_inc(gcn_in, 16)
            g.memset(ident[:, :], 0.0).then_inc(made, 1)
            g.memset(half_of[:, :], 0.0).then_inc(made, 1)
            g.memset(pick_f[:, :, :], 0.0).then_inc(made, 1)
            g.memset(minus_half[:, :], -0.5).then_inc(made, 1)
            pool.wait_ge(made, 4)
            g.affine_select(out=ident[:, :], in_=ident[:, :], compare_op=ALU.not_equal, fill=1.0, base=0,
                            pattern=[[-1, 128]], channel_multiplier=1).then_inc(made, 1)
            g.memset(half_of[0:64, 0:1], 1.0).then_inc(made, 1)
            pool.wait_ge(made, 6)
            g.memset(half_of[64:128, 1:2], 1.0).then_inc(made, 1)
            pool.wait_ge(made, 7)
            for r in range(2):
                pool.wait_ge(made, 7 + r)
                rows = pick_f[32 * r:32 * r + 8, :, :].rearrange("p t (e d) -> p t e d", d=DH)
                g.affine_select(out=rows, in_=rows, compare_op=ALU.not_equal, fill=1.0, base=0,
                                pattern=[[-2, PAIRS1], [-1, 2], [0, DH]], channel_multiplier=1).then_inc(made, 1)
            pool.sem_inc(res_added, PAIRS1)
            pool.sem_inc(nlow_done, 2)

            def rstd_of(k):
                pool.wait_ge(stat_done, 4 * k + 4)
                pool.sem_inc(passed_gpsimd, 1)
                g.tensor_scalar(var_e[:, :], mv[:, :, 1], 1.0, LN_EPS, ALU.mult, ALU.add).then_inc(var_done, 1)
                pool.wait_ge(var_done, 4 * k + 1)
                pool.sem_inc(passed_gpsimd, 1)
                g.tensor_tensor(rstd[:, :], var_e[:, :], minus_half[:, 0:C], ALU.pow).then_inc(var_done, 1)
                pool.wait_ge(var_done, 4 * k + 2)
                pool.sem_inc(passed_gpsimd, 1)
                g.tensor_tensor(mr[:, :], mv[:, :, 0], rstd[:, :], ALU.mult).then_inc(var_done, 1)
                pool.wait_ge(var_done, 4 * k + 3)
                pool.sem_inc(passed_gpsimd, 1)
                g.tensor_scalar(shift[:, :], mr[:, :], -1.0, 0.0, ALU.mult, ALU.add).then_inc(var_done, 1)

            rstd_of(0)

            def body(a, n, more):
                if n is not None:
                    pool.wait_ge(adj_loaded, 16 * n + 16)
                    pool.sem_inc(passed_gpsimd, 1)
                    if a is not None:
                        pool.wait_ge(turn_done, out_of_psum(a, "s3"))
                        pool.sem_inc(passed_gpsimd, 1)
                    g.tensor_scalar(mask0[:, :, :], adj8[:, :, :], FLT_MAX, -FLT_MAX, ALU.mult, ALU.add).then_inc(mask0_ready, 1)
                    if a is None:
                        pool.wait_ge(small_in, 64)
                        pool.wait_ge(stage_lo, len(PIECES))
                    else:
                        pool.wait_ge(res_moved, 16 * a + 16)
                        pool.wait_ge(h_ready, 4 * a + 4)
                    pool.wait_ge(x_loaded, 16 * n + 16)
                    for c in range(C):
                        g.tensor_tensor(x_mid[:, c, :], x_in[:, c, :], bias_o[:, :], ALU.add).then_inc(mid_ready, 1)
                for s in steps(a, n, more):
                    kind, p = s if isinstance(s, tuple) else (s, None)
                    if kind == "back":
                        pool.wait_ge(rel_done, pairs(a, p) + 1)
                        if p == 0:
                            pool.wait_ge(res_moved, 16 * a + 16)
                        part = x_res[:, :, 128 * p:128 * p + 128]
                        g.tensor_tensor(part, part, rel[:, :, :], ALU.add).then_inc(res_added, 1)
                    elif kind[:3] == "sum":
                        hd = int(kind[3])
                        pool.wait_ge(rsum0_done, H0 * n + hd + 1)
                        pool.sem_inc(passed_gpsimd, 1)
                        for c in range(C):
                            last = g.tensor_scalar(prob0[:, hd, c, :], prob0[:, hd, c, :], rsum0[:, hd, c:c + 1], 0.0, ALU.mult, ALU.add)
                        last.then_inc(norm0_done, 1)
                    elif kind == "wo1":
                        rstd_of(2 * n + 1)
                    elif kind in ("m0", "m1", "m2", "m3"):
                        t = int(kind[1])
                        pool.wait_ge(turn_done, out_of_psum(n, kind))
                        g.tensor_tensor(msq[:, t, :], m32[:, t, :], m32[:, t, :], ALU.mult).then_inc(msq_done, 1)
                    elif kind == "rt":
                        if a is not None:
                            pool.wait_ge(masked, pairs(a, PAIRS1, 4))
                            pool.wait_ge(fac_steps, pairs(a, PAIRS1, 3))
                            pool.sem_inc(passed_gpsimd, 1)
                        g.tensor_scalar(mask1[:, :, :], adj8[:, :, :], MASKED_L1, 0.0, ALU.mult, ALU.add).then_inc(mask1_ready, 1)
                        for c in range(C):
                            first = adj8[:, c, 0:2]
                            last = g.tensor_scalar(keep[:, c, 0:1], first[:, 0:1], -1.0, 1.0, ALU.mult, ALU.add)
                            last = g.tensor_scalar(keep[:, c, 1:2], first[:, 0:1], -1.0, 1.0, ALU.mult, ALU.add)
                        last.then_inc(keep_ready, 1)
                    elif kind == "rstd0":
                        rstd_of(2 * n + 2)
                    elif kind == "ss":
                        pool.wait_ge(turn_done, out_of_psum(n, "ss"))
                        g.tensor_tensor(rn[:, :], ssq[:, :], minus_half[:, :], ALU.pow).then_inc(rn_done, 1)
                    elif kind in ("bc0", "bc1"):
                        b = int(kind[2])
                        pool.wait_ge(nhigh_done, 2 * n + b + 1)
                        g.tensor_tensor(nrm[:, 1, 2 * b:2 * b + 2, :], m32[:, 2 * b:2 * b + 2, :],
                                        nrm[:, 0, 2 * b:2 * b + 2, :].bitcast(F32), ALU.subtract).then_inc(nlow_done, 1)

            rounds(pool, body)

        @block.scalar
        def _(act):
            s_ = nc.scalar
            for k, (src, dst) in enumerate(PIECES):
                act.wait_ge(stage_in[k % 4], 16 * (k // 4) + 16)
                s_.activation(flat(dst[0]), stage[k % 4], ACT.Copy).then_inc(stage_hi, 1)
            for kt in range(KT):
                act.wait_ge(fold_full, kt + 1)
                s_.activation(w_v[:, 0, kt, :], bank[kt][:, :], ACT.Copy).then_inc(fold_hi, 1)
            act.sem_inc(exp1_done, 4 * PAIRS1)
            act.sem_inc(uT_ready, 2 * PAIRS1)
            act.sem_inc(oT1_ready, PAIRS1)

            def relu_norm(k, src):
                act.wait_ge(var_done, 4 * k + 4)
                for c in range(C):
                    s_.activation(h[:, c, :], src[:, c, :], ACT.Relu, bias=shift[:, c:c + 1], scale=rstd[:, c:c + 1]).then_inc(h_ready, 1)

            relu_norm(0, x_in)
            act.wait_ge(small_in, 64)

            def body(a, n, more):
                for s in steps(a, n, more):
                    kind, p = s if isinstance(s, tuple) else (s, None)
                    if kind == "relu1":
                        relu_norm(2 * n + 1, x_mid)
                    elif kind == "relu0":
                        relu_norm(2 * n + 2, x_in)
                    elif kind == "exp":
                        for e in range(2):
                            for c in range(C):
                                act.wait_ge(masked, pairs(a, p, 4) + 2 * e + c + 1)
                                e_sl = att[:, p % 2, e, c, :]
                                s_.activation(e_sl, e_sl, ACT.Exp, bias=nmax1[:, p, c, e:e + 1], scale=-1.0,
                                              accum_out=esum1[:, p, c, e:e + 1]).then_inc(exp1_done, 1)
                    elif kind == "turn":
                        for e in range(2):
                            act.wait_ge(t_full, pairs(a, p, 2) + e + 1)
                            act.wait_ge(uv_full, pairs(a, p))
                            s_.activation(uT[:, e, :], t_bank[e][:, :], ACT.Copy).then_inc(uT_ready, 1)
                    elif kind == "value":
                        act.wait_ge(uv_full, pairs(a, p) + 1)
                        act.wait_ge(o_full, pairs(a, p))
                        s_.activation(oT1[:, :], t_bank[0][:, 0:N], ACT.Copy).then_inc(oT1_ready, 1)
                    elif kind[:2] == "ht" or kind in ("qk0", "qk1", "av"):
                        act.wait_ge(turn_full, in_psum(n, kind))
                        dst = (hT[:, 0, 2 * "ab".index(kind[3]):2 * "ab".index(kind[3]) + 2, :] if kind[:2] == "ht" else
                               oT0[:, 0, :, :] if kind == "av" else qkm[:, 0, 2 * int(kind[2]):2 * int(kind[2]) + 2, :])
                        s_.activation(flat(dst), bank[bank_of[kind]][:, :], ACT.Copy).then_inc(high_done, 1)
                    elif kind in ("exp0", "exp1", "exp2", "exp3"):
                        hd = int(kind[3])
                        act.wait_ge(turn_done, out_of_psum(n, f"s{hd}"))
                        for c in range(C):
                            last = s_.activation(prob0[:, hd, c, :], prob0[:, hd, c, :], ACT.Exp, bias=nmax0[:, hd, c:c + 1], scale=-1.0,
                                                 accum_out=esum0[:, hd, c:c + 1])
                        last.then_inc(exp0_done, 1)
                    elif kind[:2] == "pt":
                        if kind == "pt0":
                            act.wait_ge(nlow_done, 2 * n + 2)
                        act.wait_ge(turn_full, in_psum(n, kind))
                        s_.activation(ptm[:, int(kind[2]), :], bank[bank_of[kind]][:, :], ACT.Copy).then_inc(pT_ready, 1)
                    elif kind[0] in "mqk" and kind[1].isdigit():
                        t = int(kind[1])
                        dst, bias = {"m": (qkm, bias_m), "q": (q1, bias_q), "k": (k1, bias_k)}[kind[0]]
                        act.wait_ge(turn_full, in_psum(n, kind))
                        s_.activation(dst[:, 0, t, :], bank[bank_of[kind]][:, 0:N], ACT.Identity, bias=bias[:, t:t + 1]).then_inc(high_done, 1)
                    elif kind in ("bc0", "bc1"):
                        b = int(kind[2])
                        act.wait_ge(turn_done, out_of_psum(n, kind))
                        s_.activation(flat(nrm[:, 0, 2 * b:2 * b + 2, :]), flat(m32[:, 2 * b:2 * b + 2, :]), ACT.Copy).then_inc(nhigh_done, 1)

            rounds(act, body)

        @block.vector
        def _(dve):
            v_ = nc.vector
            dve.wait_ge(made, 9)
            v_.tensor_copy(pick[:, :, :], pick_f[:, :, :]).then_inc(pick_made, 1)
            v_.memset(rnT[:, :].bitcast(F32), 0.0).then_inc(pick_made, 1)
            dve.wait_ge(gcn_in, 64)
            v_.tensor_copy(gcn_bb[:, :, :], gcn_b[:, :].rearrange("p (h o) -> p h o", o=1).to_broadcast([64, H1, 128])).then_inc(pick_made, 1)
            dve.sem_inc(turn_done, len(BY_VECTOR))
            dve.sem_inc(masked, 4 * PAIRS1)
            dve.sem_inc(gated, 4 * PAIRS1)
            dve.sem_inc(fac_steps, 3 * PAIRS1)
            dve.sem_inc(rel_done, PAIRS1)

            def row_stats(src, c):
                v_.bn_stats(stats[:, c, :], src[:, c, :]).then_inc(stat_done, 1)

            def mean_var(k):
                for c in range(C):
                    dve.wait_ge(stat_done, 4 * k + c + 1)
                    dve.sem_inc(passed_vector, 1)
                    v_.bn_aggr(mv[:, c, :], stats[:, c, :]).then_inc(stat_done, 1)

            dve.wait_ge(x_loaded, 16)
            row_stats(x_in, 0)
            row_stats(x_in, 1)
            mean_var(0)
            for k, (src, dst) in enumerate(PIECES):
                dve.wait_ge(stage_hi, k + 1)
                v_.tensor_tensor(flat(dst[1]), stage[k % 4], flat(dst[0]).bitcast(F32), ALU.subtract).then_inc(stage_lo, 1)
            for kt in range(KT):
                dve.wait_ge(fold_hi, kt + 1)
                v_.tensor_tensor(w_v[:, 1, kt, :], bank[kt][:, :], w_v[:, 0, kt, :].bitcast(F32), ALU.subtract).then_inc(fold_done, 1)
            dve.wait_ge(fold_full, KT + 1)
            v_.tensor_copy(bias_v[:, :], bank[KT][:, :]).then_inc(fold_done, 1)
            dve.wait_ge(small_in, 64)
            dve.wait_ge(fold_done, KT + 1)

            def body(a, n, more):
                for s in steps(a, n, more):
                    kind, p = s if isinstance(s, tuple) else (s, None)
                    if kind in BY_VECTOR:
                        full = bank[bank_of[kind]]
                        if kind in ("s0", "s1", "s2", "s3"):
                            if kind == "s0":
                                dve.wait_ge(mask0_ready, n + 1)
                            dve.wait_ge(turn_full, in_psum(n, kind))
                            dve.sem_inc(passed_vector, 1)
                        else:
                            dve.wait_ge(turn_full, in_psum(n, kind))
                        if kind in HIGHS:
                            dve.wait_ge(high_done, len(HIGHS) * n + HIGHS.index(kind) + 1)
                    if kind == "score":
                        dve.wait_ge(score_full, pairs(a, p) + 1)
                        if p == 0:
                            dve.wait_ge(mask1_ready, a + 1)
                        dve.wait_ge(t_full, pairs(a, p, 2) - 2)
                        dve.sem_inc(passed_vector, 1)
                        for e in range(2):
                            for c in range(C):
                                v_.tensor_tensor_reduce(out=att[:, p % 2, e, c, :], in0=score_bank[e][:, c * N:c * N + N], in1=mask1[:, c, :],
                                                        scale=-SCALE, scalar=FLT_MAX, op0=ALU.add, op1=ALU.min,
                                                        accum_out=nmax1[:, p, c, e:e + 1]).then_inc(masked, 1)
                    elif kind == "cos":
                        dve.wait_ge(gram_full, pairs(a, p) + 1)
                        for e in range(2):
                            for c in range(C):
                                dve.wait_ge(exp1_done, pairs(a, p, 4) + 2 * e + c + 1)
                                e_sl = att[:, p % 2, e, c, :]
                                v_.scalar_tensor_tensor(e_sl, gram_bank[e][:, c * N:c * N + N], COS_THRESHOLD, e_sl, ALU.is_gt, ALU.mult,
                                                        accum_out=usum1[:, p, c, e:e + 1]).then_inc(gated, 1)
                    elif kind == "factor":
                        dve.wait_ge(gated, pairs(a, p, 4) + 4)
                        v_.tensor_tensor(den1[:, :, :], esum1[:, p, :, :], usum1[:, p, :, :], ALU.add).then_inc(fac_steps, 1)
                        dve.wait_ge(fac_steps, pairs(a, p, 3) + 1)
                        v_.reciprocal(rec1[:, :, :], den1[:, :, :]).then_inc(fac_steps, 1)
                        dve.wait_ge(fac_steps, pairs(a, p, 3) + 2)
                        dve.wait_ge(keep_ready, a + 1)
                        v_.tensor_tensor(fac1[:, :, :], rec1[:, :, :], keep[:, :, :], ALU.mult).then_inc(fac_steps, 1)
                    elif kind == "back":
                        dve.wait_ge(fac_steps, pairs(a, p, 3) + 3)
                        dve.wait_ge(o_full, pairs(a, p) + 1)
                        dve.wait_ge(res_added, pairs(a, p))
                        v_.scalar_tensor_tensor(rel[:, :, :].rearrange("p c (e d) -> p (c e) d", d=DH),
                                                t_bank[1][:, 0:N].rearrange("p (x d) -> p x d", d=DH), 0.0,
                                                fac1[:, :, :].rearrange("p c (e o) -> p (c e) o", o=1).to_broadcast([128, 2 * C, DH]),
                                                ALU.max, ALU.mult).then_inc(rel_done, 1)
                    elif kind[:2] == "ht":
                        t = 2 * "ab".index(kind[3])
                        v_.tensor_tensor(flat(hT[:, 1, t:t + 2, :]), full[:, :], flat(hT[:, 0, t:t + 2, :]).bitcast(F32), ALU.subtract).then_inc(turn_done, 1)
                    elif kind in ("qk0", "qk1"):
                        t = 2 * int(kind[2])
                        v_.tensor_tensor(flat(qkm[:, 1, t:t + 2, :]), full[:, :], flat(qkm[:, 0, t:t + 2, :]).bitcast(F32), ALU.subtract).then_inc(turn_done, 1)
                    elif kind == "v0":
                        v_.tensor_copy(flat(v0[:, :, :]), full[:, :]).then_inc(turn_done, 1)
                    elif kind in ("s0", "s1", "s2", "s3"):
                        hd = int(kind[1])
                        for c in range(C):
                            last = v_.tensor_tensor_reduce(out=prob0[:, hd, c, :], in0=full[:, c * N:c * N + N], in1=mask0[:, c, :],
                                                           scale=-SCALE, scalar=FLT_MAX, op0=ALU.add, op1=ALU.min,
                                                           accum_out=nmax0[:, hd, c:c + 1])
                        last.then_inc(turn_done, 1)
                    elif kind[:3] == "sum":
                        hd = int(kind[3])
                        dve.wait_ge(exp0_done, H0 * n + hd + 1)
                        v_.reciprocal(rsum0[:, hd, :], esum0[:, hd, :]).then_inc(rsum0_done, 1)
                    elif kind == "av":
                        v_.tensor_tensor(flat(oT0[:, 1, :, :]), full[:, :], flat(oT0[:, 0, :, :]).bitcast(F32), ALU.subtract).then_inc(turn_done, 1)
                    elif kind in ("wo0", "wo1"):
                        c = int(kind[2])
                        dve.wait_ge(mid_ready, 2 * n + c + 1)
                        v_.tensor_tensor(x_mid[:, c, :], full[:, :], x_mid[:, c, :], ALU.add).then_inc(turn_done, 1)
                        dve.wait_ge(turn_done, out_of_psum(n, kind))
                        row_stats(x_mid, c)
                        if c == 1:
                            mean_var(2 * n + 1)
                    elif kind in ("m0", "m1", "m2", "m3"):
                        t = int(kind[1])
                        v_.tensor_scalar(m32[:, t, :], full[:, 0:N], bias_m[:, t:t + 1], None, ALU.add)
                        v_.scalar_tensor_tensor(qkm[:, 1, t, :], full[:, 0:N], bias_m[:, t:t + 1], qkm[:, 0, t, :].bitcast(F32),
                                                ALU.add, ALU.subtract).then_inc(turn_done, 1)
                    elif kind == "stats0":
                        dve.wait_ge(x_loaded, 16 * n + 32)
                        row_stats(x_in, 0)
                        row_stats(x_in, 1)
                        mean_var(2 * n + 2)
                    elif kind in ("vv0", "vv1"):
                        v_.tensor_tensor(v1[:, int(kind[2]), :], full[:, :], bias_v[:, :], ALU.add).then_inc(turn_done, 1)
                    elif kind[0] in "qk" and kind[1].isdigit():
                        t = int(kind[1])
                        dst, bias = {"q": (q1, bias_q), "k": (k1, bias_k)}[kind[0]]
                        v_.scalar_tensor_tensor(dst[:, 1, t, :], full[:, 0:N], bias[:, t:t + 1], dst[:, 0, t, :].bitcast(F32),
                                                ALU.add, ALU.subtract).then_inc(turn_done, 1)
                    elif kind == "ss":
                        v_.tensor_scalar(ssq[:, :], full[:, 0:C * H1], COS_EPS * COS_EPS, None, ALU.max).then_inc(turn_done, 1)
                    elif kind == "rt":
                        v_.tensor_copy(rnT[0:H1, :], full[0:H1, 0:N]).then_inc(rt_high, 1)
                        dve.wait_ge(rt_high, n + 1)
                        v_.tensor_tensor(rnT[32:32 + H1, :], full[0:H1, 0:N], rnT[0:H1, :].bitcast(F32), ALU.subtract).then_inc(turn_done, 1)
                    elif kind in ("bc0", "bc1"):
                        t = 2 * int(kind[2])
                        v_.tensor_tensor(flat(m32[:, t:t + 2, :]), full[:, :], flat(m32[:, t:t + 2, :]), ALU.mult).then_inc(turn_done, 1)

            rounds(dve, body)

        @block.tensor
        def _(pe):
            t_ = nc.tensor
            pe.wait_ge(made, 9)
            pe.wait_ge(pick_made, 3)
            for kt in range(KT):
                for hd in range(H1):
                    rows = gcn_rows[hd // 4].rearrange("p (h d) -> p h d", d=D)
                    last = t_.matmul(bank[kt][:, hd * DH:hd * DH + DH], rows[:, hd % 4, kt * 128:kt * 128 + 128], gcn_w[:, :], start=True, stop=True)
                last.then_inc(fold_full, 1)
            for hd in range(H1):
                last = t_.matmul(bank[KT][:, hd * DH:hd * DH + DH], gcn_bb[:, hd, :], gcn_w[:, :], start=True, stop=True)
            last.then_inc(fold_full, 1)
            pe.wait_ge(fold_done, KT + 1)
            pe.wait_ge(stage_lo, len(PIECES))
            pe.sem_inc(score_full, PAIRS1)
            pe.sem_inc(gram_full, PAIRS1)
            pe.sem_inc(t_full, 2 * PAIRS1)
            pe.sem_inc(uv_full, PAIRS1)
            pe.sem_inc(o_full, PAIRS1)

            def transposes(dst, src_of):
                for outer in range(2):
                    for c in range(C):
                        b = 2 * outer + c
                        last = t_.transpose(dst[:, b * 128:b * 128 + 128], src_of(outer, c), ident[:, :])
                return last

            def project(dst, w, t, rhs):
                for k in range(KT):
                    for i, (ws, rs) in enumerate(PASSES):
                        last = t_.matmul(dst, w(ws, k)[:, t * 128:t * 128 + 128], rhs[:, rs, k, :],
                                         start=(k == 0 and i == 0), stop=(k == KT - 1 and i == 2))
                return last

            def project_rows(dst, lhs, chunks, c, w):
                for k in range(chunks):
                    for i, (ls, ws) in enumerate(PASSES):
                        last = t_.matmul(dst, lhs[:, ls, k, c * 128:c * 128 + 128], w(ws, k),
                                         start=(k == 0 and i == 0), stop=(k == chunks - 1 and i == 2))
                return last

            def head_products(banks, left, right):
                last = [None, None]
                for c in range(C):
                    for i, (ls, rs) in enumerate(PASSES):
                        for e in range(2):
                            r = slice(64 * e, 64 * e + 64)
                            last[e] = t_.matmul(banks[e][:, c * N:c * N + N], left[r, ls, c * 128:c * 128 + 128], right[r, rs, :],
                                                start=(i == 0), stop=(i == 2))
                return last

            def values(dst, v, hd0, rhs):
                for jc in range(C):
                    for e in range(2):
                        last = t_.matmul(dst[64 * e:64 * e + 64, :], v[:, jc, (hd0 + e) * DH:(hd0 + e + 1) * DH], rhs(e, jc),
                                         start=(jc == 0), stop=(jc == C - 1))
                return last

            def body(a, n, more):
                for s in steps(a, n, more):
                    kind, p = s if isinstance(s, tuple) else (s, None)
                    if kind in PRODUCTS:
                        full = bank[bank_of[kind]]
                    if kind == "score":
                        pe.wait_ge(turn_done, out_of_psum(a, f"k{p}"))
                        pe.wait_ge(masked, pairs(a, p, 4))
                        head_products(score_bank, q1[:, :, p, :], k1[:, :, p, :])[1].then_inc(score_full, 1)
                    elif kind == "cos":
                        pe.wait_ge(nlow_done, 2 * a + 2 + p // 2 + 1)
                        if p == 0:
                            pe.wait_ge(turn_done, out_of_psum(a, "bc1"))
                        pe.wait_ge(gated, pairs(a, p, 4))
                        head_products(gram_bank, nrm[:, :, p, :], nrm[:, :, p, :])[1].then_inc(gram_full, 1)
                    elif kind == "turn":
                        for e in range(2):
                            pe.wait_ge(gated, pairs(a, p, 4) + 2 * e + 2)
                            if e == 0:
                                pe.wait_ge(oT1_ready, pairs(a, p))
                            else:
                                pe.wait_ge(rel_done, pairs(a, p))
                            transposes(t_bank[e], lambda jc, c: att[:, p % 2, e, c, jc * 128:jc * 128 + 128]).then_inc(t_full, 1)
                    elif kind == "value":
                        pe.wait_ge(uT_ready, pairs(a, p, 2) + 2)
                        if p == 0:
                            pe.wait_ge(turn_done, out_of_psum(a, "vv1"))
                        values(t_bank[0][:, 0:N], v1, 2 * p, lambda e, jc: uT[:, e, jc * N:jc * N + N]).then_inc(uv_full, 1)
                    elif kind == "back":
                        pe.wait_ge(oT1_ready, pairs(a, p) + 1)
                        for c in range(C):
                            last = t_.transpose(t_bank[1][:, c * 128:c * 128 + 128], oT1[:, c * 128:c * 128 + 128], ident[:, :])
                        last.then_inc(o_full, 1)
                    elif kind[:2] == "ht":
                        t = 2 * "ab".index(kind[3])
                        pe.wait_ge(h_ready, 4 * n + (2 if kind[2] == "0" else 4))
                        pe.wait_ge(turn_done, room(n, kind))
                        transposes(full, lambda k, c: h[:, c, (t + k) * 128:(t + k + 1) * 128]).then_inc(turn_full, 1)
                    elif kind in ("qk0", "qk1"):
                        w = int(kind[2])
                        pe.wait_ge(turn_done, out_of_psum(n, "ht0b"))
                        pe.wait_ge(turn_done, room(n, kind))
                        for t in range(2):
                            last = project(full[:, t * N:t * N + N], lambda s2, k: w_qkv[:, s2, w, k, :], t, hT)
                        last.then_inc(turn_full, 1)
                    elif kind == "v0":
                        pe.wait_ge(turn_done, out_of_psum(n, "ht0b"))
                        pe.wait_ge(turn_done, room(n, kind))
                        for c in range(C):
                            last = project_rows(full[:, c * INNER:c * INNER + INNER], hT, KT, c, lambda s2, k: w_qkv[:, s2, 2, k, :])
                        last.then_inc(turn_full, 1)
                    elif kind in ("s0", "s2"):
                        t = int(kind[1]) // 2
                        pe.wait_ge(turn_done, room(n, f"s{2 * t + 1}"))
                        pair_banks = [full, bank[bank_of[f"s{2 * t + 1}"]]]
                        for last in head_products(pair_banks, qkm[:, :, t, :], qkm[:, :, 2 + t, :]):
                            last.then_inc(turn_full, 1)
                    elif kind[:2] == "pt":
                        hd = int(kind[2])
                        pe.wait_ge(norm0_done, H0 * n + hd + 1)
                        if hd < 2:
                            pe.wait_ge(turn_done, room(n, kind))
                        else:
                            pe.wait_ge(pT_ready, H0 * n + hd - 1)
                        transposes(full, lambda jc, c: prob0[:, hd, c, jc * 128:jc * 128 + 128]).then_inc(turn_full, 1)
                    elif kind == "av":
                        pe.wait_ge(pT_ready, H0 * n + H0)
                        for t in range(PAIRS0):
                            last = values(full[:, t * N:t * N + N], v0, 2 * t, lambda e, jc: ptm[:, 2 * t + e, jc * N:jc * N + N])
                        last.then_inc(turn_full, 1)
                    elif kind in ("wo0", "wo1"):
                        pe.wait_ge(turn_done, out_of_psum(n, "av"))
                        project_rows(full[:, :], oT0, PAIRS0, int(kind[2]), lambda s2, k: w_o[:, s2, k, :]).then_inc(turn_full, 1)
                    elif kind in ("m0", "m1", "m2", "m3"):
                        pe.wait_ge(turn_done, out_of_psum(n, "ht1b"))
                        pe.wait_ge(turn_done, room(n, kind))
                        project(full[:, 0:N], lambda s2, k: w_map[:, s2, k, :], int(kind[1]), hT).then_inc(turn_full, 1)
                    elif kind in ("vv0", "vv1"):
                        pe.wait_ge(turn_done, out_of_psum(n, "ht1b"))
                        pe.wait_ge(turn_done, room(n, kind))
                        project_rows(full[:, :], hT, KT, int(kind[2]), lambda s2, k: w_v[:, s2, k, :]).then_inc(turn_full, 1)
                    elif kind[0] in "qk" and kind[1].isdigit():
                        pe.wait_ge(turn_done, out_of_psum(n, "m3"))
                        pe.wait_ge(turn_done, room(n, kind))
                        w = {"q": w_q, "k": w_k}[kind[0]]
                        project(full[:, 0:N], lambda s2, k: w[:, s2, k, :], int(kind[1]), qkm).then_inc(turn_full, 1)
                    elif kind == "ss":
                        pe.wait_ge(msq_done, KT * n + KT)
                        if a is not None:
                            pe.wait_ge(masked, pairs(a, PAIRS1, 4))
                        for t in range(KT):
                            for c in range(C):
                                last = t_.matmul(full[:, c * H1 + 2 * t:c * H1 + 2 * t + 2], msq[:, t, c * 128:c * 128 + 128], half_of[:, :], start=True, stop=True)
                        last.then_inc(turn_full, 1)
                    elif kind == "rt":
                        pe.wait_ge(rn_done, n + 1)
                        for c in range(C):
                            last = t_.transpose(full[0:H1, c * 128:c * 128 + 128], rn[:, c * H1:c * H1 + H1], ident[:, :])
                        last.then_inc(turn_full, 1)
                    elif kind in ("bc0", "bc1"):
                        pe.wait_ge(turn_done, out_of_psum(n, "rt"))
                        if a is not None:
                            pe.wait_ge(gated, pairs(a, PAIRS1, 4))
                        for t in range(2):
                            last = t_.matmul(full[:, t * N:t * N + N], pick[:, 2 * int(kind[2]) + t, :], rnT[:, :], start=True, stop=True)
                        last.then_inc(turn_full, 1)

            rounds(pe, body)


def build(nc, args):
    gnn_two_layers(nc, *args)


def kernel(x, adj, L0_gnn_Wq, L0_gnn_Wk, L0_gnn_Wv, L0_gnn_Wo, L0_gnn_bo, L1_gnn_map_w, L1_gnn_map_b, L1_gnn_q_w,
           L1_gnn_q_b, L1_gnn_k_w, L1_gnn_k_b, L1_gnn_gcn_map_w, L1_gnn_gcn_map_b, L1_gnn_gcn_W):
    import concourse.bacc as bacc
    from concourse.bass_utils import run_bass_kernel_spmd

    def rows(a):
        return np.ascontiguousarray(a)

    arrays = {
        "x": rows(x), "adj": rows(adj),
        "wq": rows(L0_gnn_Wq), "wk": rows(L0_gnn_Wk), "wv": rows(L0_gnn_Wv), "wo": rows(L0_gnn_Wo), "bo": rows(L0_gnn_bo),
        "map_t": rows(np.asarray(L1_gnn_map_w).T), "map_b": rows(L1_gnn_map_b),
        "q_t": rows(np.asarray(L1_gnn_q_w).T), "q_b": rows(L1_gnn_q_b),
        "k_t": rows(np.asarray(L1_gnn_k_w).T), "k_b": rows(L1_gnn_k_b),
        "gcn_map": rows(L1_gnn_gcn_map_w), "gcn_map_b": rows(L1_gnn_gcn_map_b),
        "gcn_t": rows(np.asarray(L1_gnn_gcn_W).T),
    }
    nc = bacc.Bacc("TRN2", target_bir_lowering=False, num_devices=1)
    args = [nc.dram_tensor(n, a.shape, mybir.dt.from_np(a.dtype), kind="ExternalInput").ap() for n, a in arrays.items()]
    args.append(nc.dram_tensor("out", arrays["x"].shape, F32, kind="ExternalOutput").ap())
    build(nc, args)
    r = run_bass_kernel_spmd(nc, [arrays], core_ids=[0])
    return r.results[0]["out"]
```

```python
from contextlib import ExitStack

import numpy as np
import concourse.bass as bass
from concourse import mybir

F32 = mybir.dt.float32
F32R = mybir.dt.float32r
U8 = mybir.dt.uint8
ALU = mybir.AluOpType
ACT = mybir.ActivationFunctionType

PASSES = ((0, 0), (0, 1), (1, 0))
LN_EPS = 1e-5
COS_EPS = 1e-8
COS_THRESHOLD = 0.1
MASKED_L1 = -1e10
FLT_MAX = float(np.finfo(np.float32).max)


def gnn_two_layers(nc, x, adj, wq, wk, wv, wo, bo, map_t, map_b, q_t, q_b, k_t, k_b, gcn_map, gcn_map_b, gcn_t, out):
    G, N, D = x.shape
    C = N // 128
    KT = D // 128
    DH = 64
    INNER = wq.shape[1]
    H0, H1 = INNER // DH, D // DH
    PAIRS0, PAIRS1 = H0 // 2, H1 // 2
    SCALE = DH ** -0.5
    assert (C, KT, H0, H1) == (2, 4, 4, 8)

    ORDER = ["ht0a", "ht0b", ("unit", 0), ("unit", 1), ("score", 0), "qk0", "mask0", "qk1", "qk2", "s0", "s1",
             "exp0", "qk3", ("exp_a", 0), ("exp_b", 0), "v0", ("cos", 0), "mid", "exp1", "s2", "sum0", ("turn", 0),
             "exp2", ("factor", 0), "s3", "exp3", ("score", 1), "sum1", ("value", 0), ("exp_a", 1), ("exp_b", 1),
             "sum2", ("cos", 1), "pt0", "pt1", "sum3", ("back", 0), "pt2", ("turn", 1), "pt3", ("score", 2), "av",
             ("value", 1), ("exp_a", 2), ("factor", 1), ("exp_b", 2), ("back", 1), "wo0", ("cos", 2), "wo1",
             ("factor", 2), ("turn", 2), "norm1", ("score", 3), ("value", 2), ("back", 2), "ht1a", "ht1b",
             ("exp_a", 3), ("exp_b", 3), ("cos", 3), "m0", ("turn", 3), "m1", "m2", "stats0", ("value", 3), "vv0",
             ("factor", 3), "rstd0", "m3", "vv1", "q0", "norm0", "k0", "ss", "q1", ("back", 3), "q2", "k1", "rt",
             "q3", "k2", "bc0", "bc1", "k3"]
    PRODUCTS = [s for s in ORDER if isinstance(s, str) and s[:3] not in ("exp", "sum", "sta", "rst", "nor", "mas", "mid")]
    BORROWED = {"ht0a": 4, "ht0b": 5, "s0": 4, "s1": 5, "ss": 0, "rt": 1, "bc0": 2, "bc1": 3}
    LONG = [s for s in PRODUCTS if s not in BORROWED]
    assert len(LONG) % 2 == 0
    bank_of = BORROWED | {s: 6 + k % 2 for k, s in enumerate(LONG)}
    BY_VECTOR = [s for s in PRODUCTS if s[:2] != "pt"]
    HIGHS = [s for s in PRODUCTS if s[:2] in ("ht", "qk", "av") or (s[0] in "mqk" and s[1].isdigit())]

    def in_psum(n, name):
        return len(PRODUCTS) * n + PRODUCTS.index(name) + 1

    def out_of_psum(n, name):
        return len(BY_VECTOR) * (n + 1) + BY_VECTOR.index(name) + 1

    def room(n, name):
        k = LONG.index(name) - 2
        return out_of_psum(n, LONG[k]) - (0 if k >= 0 else len(BY_VECTOR))

    def pairs(a, p, steps=1):
        return steps * PAIRS1 * (a + 1) + steps * p

    ctx = ExitStack()
    with ctx:
        def sb(name, shape, dt=F32):
            return ctx.enter_context(nc.sbuf_tensor(name, shape, dt))

        w_qkv = sb("w_qkv", [128, 2, 3, KT, INNER], F32R)
        w_o = sb("w_o", [128, 2, PAIRS0, D], F32R)
        w_map = sb("w_map", [128, 2, KT, D], F32R)
        w_q = sb("w_q", [128, 2, KT, D], F32R)
        w_k = sb("w_k", [128, 2, KT, D], F32R)
        w_v = sb("w_v", [128, 2, KT, D], F32R)
        bias_o = sb("bias_o", [128, D])
        bias_v = sb("bias_v", [128, D])
        bias_m = sb("bias_m", [128, KT])
        bias_q = sb("bias_q", [128, KT])
        bias_k = sb("bias_k", [128, KT])
        ident = sb("ident", [128, 128])
        half_of = sb("half_of", [128, 2])
        pick = sb("pick", [40, PAIRS1, 128], F32R)
        minus_half = sb("minus_half", [128, 16])
        gcn_w = sb("gcn_w", [128, DH])
        gcn_b = sb("gcn_b", [128, H1 // 2])

        x_in = sb("x_in", [128, C, D])
        x_mid = sb("x_mid", [128, C, D])
        x_res = sb("x_res", [128, C, D])
        h = sb("h", [128, C, D])
        hT = sb("hT", [128, 2, KT, N], F32R)
        qkm = sb("qkm", [128, 2, KT, N], F32R)
        v0 = sb("v0", [128, C, INNER])
        prob0 = sb("prob0", [128, H0, C, N])
        ptm = sb("ptm", [128, H0, C * N])
        m32 = ptm[:, 0:2, :].rearrange("p a (b n) -> p (a b) n", n=N)
        msq = ptm[:, 2:4, :].rearrange("p a (b n) -> p (a b) n", n=N)
        oT0 = sb("oT0", [128, 2, PAIRS0, N], F32R)
        nrm = sb("nrm", [128, 2, KT, N], F32R)
        q1 = sb("q1", [128, 2, KT, N], F32R)
        k1 = sb("k1", [128, 2, KT, N], F32R)
        v1 = sb("v1", [128, C, D])
        att = sb("att", [128, 2, 2, C, N])
        uT = sb("uT", [128, 2, C * N])
        oT1 = sb("oT1", [128, N])
        pick_f = uT[0:40, 0, :].rearrange("p (t m) -> p t m", m=128)
        gcn_bb = v1[:, 0, :].rearrange("p (h m) -> p h m", m=128)
        gcn_rows = att[:, :, :, :, :].rearrange("p a b c n -> p (a b c n)").rearrange("p (h d) -> p h d", d=D)
        rel = sb("rel", [128, C, 128])
        adj8 = sb("adj8", [128, C, N], U8)
        mask0 = sb("mask0", [128, C, N])
        mask1 = sb("mask1", [128, C, N])
        keep = sb("keep", [128, C, 2])

        stats = sb("stats", [128, C, 6])
        mv = sb("mv", [128, C, 2])
        var_e = sb("var_e", [128, C])
        rstd = sb("rstd", [128, C])
        nmax0 = sb("nmax0", [128, H0, C])
        esum0 = sb("esum0", [128, H0, C])
        rsum0 = sb("rsum0", [128, H0, C])
        nmax1 = sb("nmax1", [128, PAIRS1, C, 2])
        esum1 = sb("esum1", [128, PAIRS1, C, 2])
        usum1 = sb("usum1", [128, PAIRS1, C, 2])
        den1 = sb("den1", [128, C, 2])
        rec1 = sb("rec1", [128, C, 2])
        fac1 = sb("fac1", [128, C, 2])
        ssq = sb("ssq", [128, C * H1])
        rn = sb("rn", [128, C * H1])
        rnT = sb("rnT", [40, N], F32R)

        bank = [ctx.enter_context(nc.psum_tensor(f"bank{b}", [128, 512], F32)) for b in range(8)]
        score_bank, gram_bank, t_bank = bank[0:2], bank[2:4], bank[4:6]

        def count(name):
            return ctx.enter_context(nc.semaphore(name))

        passed_sync, passed_gpsimd, passed_vector = count("passed_sync"), count("passed_gpsimd"), count("passed_vector")
        stage_in = [count(f"stage_in{k}") for k in range(4)]
        stage_hi = count("stage_hi")
        stage_lo = count("stage_lo")
        small_in = count("small_in")
        gcn_in = count("gcn_in")
        made = count("made")
        pick_made = count("pick_made")
        fold_full = count("fold_full")
        fold_half = count("fold_half")
        fold_hi = count("fold_hi")
        fold_done = count("fold_done")
        x_loaded = count("x_loaded")
        adj_loaded = count("adj_loaded")
        res_moved = count("res_moved")
        stored = count("stored")
        product_full = count("product_full")
        product_done = count("product_done")
        high_done = count("high_done")
        pT_ready = count("pT_ready")
        stat_done = count("stat_done")
        var_done = count("var_done")
        h_ready = count("h_ready")
        mask0_ready = count("mask0_ready")
        mid_ready = count("mid_ready")
        exp0_done = count("exp0_done")
        rsum0_done = count("rsum0_done")
        prob0_done = count("prob0_done")
        msq_done = count("msq_done")
        rn_done = count("rn_done")
        rt_high = count("rt_high")
        nhigh_done = count("nhigh_done")
        nlow_done = count("nlow_done")
        mask1_ready = count("mask1_ready")
        keep_ready = count("keep_ready")
        score_full = count("score_full")
        masked = count("masked")
        exp1_done = count("exp1_done")
        gram_full = count("gram_full")
        gated = count("gated")
        t_full = count("t_full")
        uT_ready = count("uT_ready")
        uv_full = count("uv_full")
        oT1_ready = count("oT1_ready")
        o_full = count("o_full")
        fac_steps = count("fac_steps")
        rel_done = count("rel_done")
        res_added = count("res_added")

        def rounds(eng, body):
            body(None, 0, True)
            with nc.Fori(0, G - 2, engines=[eng.engine], hint_back_edge=True) as a:
                body(a, a + 1, True)
            body(G - 2, G - 1, False)
            body(G - 1, None, False)

        def steps(a, n, more):
            return [s for s in ORDER if (isinstance(s, tuple) and a is not None)
                    or (isinstance(s, str) and n is not None and (more or s not in ("stats0", "rstd0", "norm0")))]

        def flat(ap):
            return ap.rearrange("p a b -> p (a b)")

        def halves(w, dst):
            v = w.rearrange("(k p) n -> p k n", p=128)
            return [(v[:, 2 * i:2 * i + 2, :], [dst[:, s, 2 * i:2 * i + 2, :] for s in range(2)]) for i in range(KT // 2)]

        PIECES = [(w.rearrange("(k p) n -> p k n", p=128), [w_qkv[:, s, i, :, :] for s in range(2)])
                  for i, w in enumerate((wq, wk, wv))]
        PIECES += [(wo.rearrange("(k p) n -> p k n", p=128), [w_o[:, s, :, :] for s in range(2)])]
        PIECES += halves(map_t, w_map) + halves(q_t, w_q) + halves(k_t, w_k)
        slots = [flat(t[:, :, :]) for t in (x_mid, x_res, v1, uT)]
        SLOT = [0, 1, 2, 3, 0, 1, 3, 1, 3, 1]
        EARLIER = [[j for j in range(k) if SLOT[j] == SLOT[k]] for k in range(len(PIECES))]
        SPLIT_AT = {"qk0": 4, "qk2": 5, "v0": 6, "s2": 7, "pt0": 8, "pt2": 9}
        FOLD_AT = {"s2": 0, "pt0": 1, "av": 2, "wo0": 3, "ht1a": 4}
        block = ctx.enter_context(nc.Block())

        @block.sync
        def _(sp):
            with nc.allow_non_contiguous_dma("small biases, once"):
                sp.dma_start(x_in[:, :, :], x[0].rearrange("(c p) d -> p c d", p=128)).then_inc(x_loaded, 16)
                sp.dma_start(adj8[:, :, :], adj[0].rearrange("(c p) j -> p c j", p=128)).then_inc(adj_loaded, 16)
                for k, (src, _) in enumerate(PIECES):
                    if EARLIER[k]:
                        sp.wait_ge(stage_lo, EARLIER[k][-1] + 1)
                        sp.sem_inc(passed_sync, 1)
                    if k == 3:
                        sp.wait_ge(pick_made, 1)
                    dst = slots[SLOT[k]].rearrange("p (a n) -> p a n", n=src.shape[2])
                    sp.dma_start(dst, src).then_inc(stage_in[SLOT[k]], 16)

            def body(a, n, more):
                if more:
                    sp.wait_ge(h_ready, 4 * n + 2)
                    sp.sem_inc(passed_sync, 1)
                    sp.wait_ge(mid_ready, 2 * n + 2)
                    sp.sem_inc(passed_sync, 1)
                    sp.dma_start(x_in[:, :, :], x[n + 1].rearrange("(c p) d -> p c d", p=128)).then_inc(x_loaded, 16)
                if a is not None:
                    sp.wait_ge(res_added, pairs(a, PAIRS1))
                    sp.sem_inc(passed_sync, 1)
                    sp.dma_start(out[a].rearrange("(c p) d -> p c d", p=128), x_res[:, :, :]).then_inc(stored, 16)
                if n is not None:
                    sp.wait_ge(product_done, out_of_psum(n, "wo1"))
                    sp.sem_inc(passed_sync, 1)
                    if a is not None:
                        sp.wait_ge(stored, 16 * a + 16)
                        sp.sem_inc(passed_sync, 1)
                    else:
                        sp.wait_ge(stage_lo, len(PIECES))
                        sp.sem_inc(passed_sync, 1)
                    sp.dma_start(x_res[:, :, :], x_mid[:, :, :]).then_inc(res_moved, 16)
                    if more:
                        sp.wait_ge(keep_ready, n + 1)
                        sp.sem_inc(passed_sync, 1)
                        sp.dma_start(adj8[:, :, :], adj[n + 1].rearrange("(c p) j -> p c j", p=128)).then_inc(adj_loaded, 16)

            rounds(sp, body)
            sp.wait_ge(stored, 16 * G)
            sp.sem_inc(passed_sync, 1)

        @block.gpsimd
        def _(pool):
            g = nc.gpsimd
            g.memset(ident[:, :], 0.0).then_inc(made, 1)
            g.memset(half_of[:, :], 0.0).then_inc(made, 1)
            g.memset(pick_f[:, :, :], 0.0).then_inc(made, 1)
            g.memset(minus_half[:, :], -0.5).then_inc(made, 1)
            pool.wait_ge(made, 4)
            g.affine_select(out=ident[:, :], in_=ident[:, :], compare_op=ALU.not_equal, fill=1.0, base=0,
                            pattern=[[-1, 128]], channel_multiplier=1).then_inc(made, 1)
            g.memset(half_of[0:64, 0:1], 1.0).then_inc(made, 1)
            pool.wait_ge(made, 6)
            g.memset(half_of[64:128, 1:2], 1.0).then_inc(made, 1)
            pool.wait_ge(made, 7)
            for r in range(2):
                pool.wait_ge(made, 7 + r)
                rows = pick_f[32 * r:32 * r + 8, :, :].rearrange("p t (e d) -> p t e d", d=DH)
                g.affine_select(out=rows, in_=rows, compare_op=ALU.not_equal, fill=1.0, base=0,
                                pattern=[[-2, PAIRS1], [-1, 2], [0, DH]], channel_multiplier=1).then_inc(made, 1)
            pool.sem_inc(res_added, PAIRS1)
            pool.sem_inc(nlow_done, 2)

            def rstd_of(k):
                pool.wait_ge(stat_done, 4 * k + 4)
                pool.sem_inc(passed_gpsimd, 1)
                g.tensor_scalar(var_e[:, :], mv[:, :, 1], 1.0, LN_EPS, ALU.mult, ALU.add).then_inc(var_done, 1)
                pool.wait_ge(var_done, 2 * k + 1)
                pool.sem_inc(passed_gpsimd, 1)
                g.tensor_tensor(rstd[:, :], var_e[:, :], minus_half[:, 0:C], ALU.pow).then_inc(var_done, 1)

            pool.wait_ge(made, 9)
            rstd_of(0)
            with nc.allow_non_contiguous_dma("small biases, once"):
                g.dma_start(bias_o[:, :], bo.partition_broadcast(128)).then_inc(small_in, 16)
                for dst, src in ((bias_m, map_b), (bias_q, q_b), (bias_k, k_b)):
                    g.dma_start(dst[:, :], src.rearrange("(k p) -> p k", p=128)).then_inc(small_in, 16)
                for half in range(2):
                    part = slice(64 * half, 64 * half + 64)
                    heads = slice(4 * half, 4 * half + 4)
                    g.dma_start(gcn_rows[part, :, :], gcn_map.rearrange("(h p) d -> p h d", p=DH)[:, heads, :]).then_inc(gcn_in, 16)
                    g.dma_start(gcn_w[part, :], gcn_t).then_inc(gcn_in, 16)
                    g.dma_start(gcn_b[part, :], gcn_map_b.rearrange("(h p) -> p h", p=DH)[:, heads]).then_inc(gcn_in, 16)

            def body(a, n, more):
                for s in steps(a, n, more):
                    kind, p = s if isinstance(s, tuple) else (s, None)
                    if kind == "mask0":
                        pool.wait_ge(adj_loaded, 16 * n + 16)
                        pool.sem_inc(passed_gpsimd, 1)
                        if a is not None:
                            pool.wait_ge(product_done, out_of_psum(a, "s3"))
                            pool.sem_inc(passed_gpsimd, 1)
                        g.tensor_scalar(mask0[:, :, :], adj8[:, :, :], FLT_MAX, -FLT_MAX, ALU.mult, ALU.add).then_inc(mask0_ready, 1)
                    elif kind == "mid":
                        if a is None:
                            pool.wait_ge(small_in, 64)
                            pool.wait_ge(stage_lo, 5)
                        else:
                            pool.wait_ge(res_moved, 16 * a + 16)
                            pool.wait_ge(h_ready, 4 * a + 4)
                        pool.wait_ge(x_loaded, 16 * n + 16)
                        for c in range(C):
                            g.tensor_tensor(x_mid[:, c, :], x_in[:, c, :], bias_o[:, :], ALU.add).then_inc(mid_ready, 1)
                    elif kind == "unit":
                        pool.wait_ge(nhigh_done, 2 * a + p + 1)
                        g.tensor_tensor(nrm[:, 1, 2 * p:2 * p + 2, :], m32[:, 2 * p:2 * p + 2, :],
                                        nrm[:, 0, 2 * p:2 * p + 2, :].bitcast(F32), ALU.subtract).then_inc(nlow_done, 1)
                    elif kind == "back":
                        pool.wait_ge(rel_done, pairs(a, p) + 1)
                        if p == 0:
                            pool.wait_ge(res_moved, 16 * a + 16)
                        part = x_res[:, :, 128 * p:128 * p + 128]
                        g.tensor_tensor(part, part, rel[:, :, :], ALU.add).then_inc(res_added, 1)
                    elif kind[:3] == "sum":
                        hd = int(kind[3])
                        pool.wait_ge(rsum0_done, H0 * n + hd + 1)
                        pool.sem_inc(passed_gpsimd, 1)
                        for c in range(C):
                            last = g.tensor_scalar(prob0[:, hd, c, :], prob0[:, hd, c, :], rsum0[:, hd, c:c + 1], 0.0, ALU.mult, ALU.add)
                        last.then_inc(prob0_done, 1)
                    elif kind == "wo1":
                        rstd_of(2 * n + 1)
                    elif kind in ("m0", "m1", "m2", "m3"):
                        t = int(kind[1])
                        pool.wait_ge(product_done, out_of_psum(n, kind))
                        g.tensor_tensor(msq[:, t, :], m32[:, t, :], m32[:, t, :], ALU.mult).then_inc(msq_done, 1)
                    elif kind == "rt":
                        if a is not None:
                            pool.wait_ge(masked, pairs(a, PAIRS1, 4))
                            pool.wait_ge(fac_steps, pairs(a, PAIRS1, 3))
                            pool.sem_inc(passed_gpsimd, 1)
                        g.tensor_scalar(mask1[:, :, :], adj8[:, :, :], MASKED_L1, 0.0, ALU.mult, ALU.add).then_inc(mask1_ready, 1)
                        for c in range(C):
                            first = adj8[:, c, 0:2]
                            last = g.tensor_scalar(keep[:, c, 0:1], first[:, 0:1], -1.0, 1.0, ALU.mult, ALU.add)
                            last = g.tensor_scalar(keep[:, c, 1:2], first[:, 0:1], -1.0, 1.0, ALU.mult, ALU.add)
                        last.then_inc(keep_ready, 1)
                    elif kind == "rstd0":
                        rstd_of(2 * n + 2)
                    elif kind == "ss":
                        pool.wait_ge(product_done, out_of_psum(n, "ss"))
                        g.tensor_tensor(rn[:, :], ssq[:, :], minus_half[:, :], ALU.pow).then_inc(rn_done, 1)

            rounds(pool, body)

        @block.scalar
        def _(act):
            s_ = nc.scalar
            def split_high(k):
                act.wait_ge(stage_in[SLOT[k]], 16 * len(EARLIER[k]) + 16)
                s_.activation(flat(PIECES[k][1][0]), slots[SLOT[k]], ACT.Copy).then_inc(stage_hi, 1)

            for k in range(4):
                split_high(k)
            act.sem_inc(exp1_done, 4 * PAIRS1)
            act.sem_inc(uT_ready, 2 * PAIRS1)
            act.sem_inc(oT1_ready, PAIRS1)


            def body(a, n, more):
                for s in steps(a, n, more):
                    kind, p = s if isinstance(s, tuple) else (s, None)
                    if a is None and kind in SPLIT_AT:
                        split_high(SPLIT_AT[kind])
                    if a is None and kind in FOLD_AT and FOLD_AT[kind] < KT:
                        act.wait_ge(fold_full, FOLD_AT[kind] + 1)
                        s_.activation(w_v[:, 0, FOLD_AT[kind], :], bank[FOLD_AT[kind]][:, :], ACT.Copy).then_inc(fold_hi, 1)
                    if kind in ("exp_a", "exp_b"):
                        e = "ab".index(kind[4])
                        for c in range(C):
                            act.wait_ge(masked, pairs(a, p, 4) + 2 * e + c + 1)
                            e_sl = att[:, p % 2, e, c, :]
                            s_.activation(e_sl, e_sl, ACT.Exp, bias=nmax1[:, p, c, e:e + 1], scale=-1.0,
                                          accum_out=esum1[:, p, c, e:e + 1]).then_inc(exp1_done, 1)
                    elif kind == "turn":
                        for e in range(2):
                            act.wait_ge(t_full, pairs(a, p, 2) + e + 1)
                            act.wait_ge(uv_full, pairs(a, p))
                            s_.activation(uT[:, e, :], t_bank[e][:, :], ACT.Copy).then_inc(uT_ready, 1)
                    elif kind == "value":
                        act.wait_ge(uv_full, pairs(a, p) + 1)
                        act.wait_ge(o_full, pairs(a, p))
                        s_.activation(oT1[:, :], t_bank[0][:, 0:N], ACT.Copy).then_inc(oT1_ready, 1)
                    elif kind[:2] == "ht":
                        t = 2 * "ab".index(kind[3])
                        act.wait_ge(product_full, in_psum(n, kind))
                        s_.activation(flat(hT[:, 0, t:t + 2, :]), bank[bank_of[kind]][:, :], ACT.Relu).then_inc(high_done, 1)
                    elif kind[:2] == "qk":
                        w, t = int(kind[2]) % 2, int(kind[2]) // 2
                        act.wait_ge(product_full, in_psum(n, kind))
                        s_.activation(qkm[:, 0, 2 * w + t, :], bank[bank_of[kind]][:, 0:N], ACT.Copy).then_inc(high_done, 1)
                    elif kind == "av":
                        act.wait_ge(product_full, in_psum(n, kind))
                        s_.activation(flat(oT0[:, 0, :, :]), bank[bank_of[kind]][:, :], ACT.Copy).then_inc(high_done, 1)
                    elif kind in ("exp0", "exp1", "exp2", "exp3"):
                        hd = int(kind[3])
                        act.wait_ge(product_done, out_of_psum(n, f"s{hd}"))
                        for c in range(C):
                            last = s_.activation(prob0[:, hd, c, :], prob0[:, hd, c, :], ACT.Exp, bias=nmax0[:, hd, c:c + 1], scale=-1.0,
                                                 accum_out=esum0[:, hd, c:c + 1])
                        last.then_inc(exp0_done, 1)
                    elif kind[:2] == "pt":
                        if kind == "pt0":
                            act.wait_ge(nlow_done, 2 * n + 2)
                        act.wait_ge(product_full, in_psum(n, kind))
                        s_.activation(ptm[:, int(kind[2]), :], bank[bank_of[kind]][:, :], ACT.Copy).then_inc(pT_ready, 1)
                    elif kind[0] in "mqk" and kind[1].isdigit():
                        t = int(kind[1])
                        dst, bias = {"m": (qkm, bias_m), "q": (q1, bias_q), "k": (k1, bias_k)}[kind[0]]
                        if a is None and kind == "m0":
                            act.wait_ge(small_in, 64)
                        act.wait_ge(product_full, in_psum(n, kind))
                        s_.activation(dst[:, 0, t, :], bank[bank_of[kind]][:, 0:N], ACT.Identity, bias=bias[:, t:t + 1]).then_inc(high_done, 1)
                    elif kind == "unit":
                        act.wait_ge(product_done, out_of_psum(a, f"bc{p}"))
                        s_.activation(flat(nrm[:, 0, 2 * p:2 * p + 2, :]), flat(m32[:, 2 * p:2 * p + 2, :]), ACT.Copy).then_inc(nhigh_done, 1)

            rounds(act, body)

        @block.vector
        def _(dve):
            v_ = nc.vector
            dve.sem_inc(product_done, len(BY_VECTOR))
            dve.sem_inc(masked, 4 * PAIRS1)
            dve.sem_inc(gated, 4 * PAIRS1)
            dve.sem_inc(fac_steps, 3 * PAIRS1)
            dve.sem_inc(rel_done, PAIRS1)

            def row_stats(src, c):
                v_.bn_stats(stats[:, c, :], src[:, c, :]).then_inc(stat_done, 1)

            def mean_var(k):
                for c in range(C):
                    dve.wait_ge(stat_done, 4 * k + c + 1)
                    dve.sem_inc(passed_vector, 1)
                    v_.bn_aggr(mv[:, c, :], stats[:, c, :]).then_inc(stat_done, 1)

            def normalise(k, src):
                dve.wait_ge(var_done, 2 * k + 2)
                for c in range(C):
                    v_.tensor_scalar(h[:, c, :], src[:, c, :], mv[:, c, 0:1], rstd[:, c:c + 1], ALU.subtract, ALU.mult).then_inc(h_ready, 1)

            dve.wait_ge(made, 9)
            v_.tensor_copy(pick[:, :, :], pick_f[:, :, :]).then_inc(pick_made, 1)
            dve.wait_ge(x_loaded, 16)
            row_stats(x_in, 0)
            row_stats(x_in, 1)
            mean_var(0)
            normalise(0, x_in)

            def split_low(k):
                high, low = PIECES[k][1]
                dve.wait_ge(stage_hi, k + 1)
                v_.tensor_tensor(flat(low), slots[SLOT[k]], flat(high).bitcast(F32), ALU.subtract).then_inc(stage_lo, 1)

            for k in range(4):
                split_low(k)

            def body(a, n, more):
                for s in steps(a, n, more):
                    kind, p = s if isinstance(s, tuple) else (s, None)
                    if a is None and kind in SPLIT_AT:
                        split_low(SPLIT_AT[kind])
                    if a is None and kind == "s0":
                        v_.memset(rnT[:, :].bitcast(F32), 0.0).then_inc(pick_made, 1)
                        dve.wait_ge(gcn_in, 96)
                        v_.tensor_copy(gcn_bb[:, :, :], gcn_b[:, :].rearrange("p (h o) -> p h o", o=1).to_broadcast([128, H1 // 2, 128])).then_inc(pick_made, 1)
                    if a is None and kind == "m0":
                        dve.wait_ge(small_in, 64)
                    if a is None and kind in FOLD_AT:
                        kt = FOLD_AT[kind]
                        if kt < KT:
                            dve.wait_ge(fold_hi, kt + 1)
                            v_.tensor_tensor(w_v[:, 1, kt, :], bank[kt][:, :], w_v[:, 0, kt, :].bitcast(F32), ALU.subtract).then_inc(fold_done, 1)
                        else:
                            dve.wait_ge(fold_full, KT + 1)
                            v_.tensor_copy(bias_v[:, :], bank[0][:, :]).then_inc(fold_done, 1)
                    if kind in BY_VECTOR:
                        full = bank[bank_of[kind]]
                        if kind in ("s0", "s1", "s2", "s3"):
                            if kind == "s0":
                                dve.wait_ge(mask0_ready, n + 1)
                            dve.wait_ge(product_full, in_psum(n, kind))
                            dve.sem_inc(passed_vector, 1)
                        else:
                            dve.wait_ge(product_full, in_psum(n, kind))
                        if kind in HIGHS:
                            dve.wait_ge(high_done, len(HIGHS) * n + HIGHS.index(kind) + 1)
                    if kind == "score":
                        dve.wait_ge(score_full, pairs(a, p) + 1)
                        if p == 0:
                            dve.wait_ge(mask1_ready, a + 1)
                        dve.wait_ge(t_full, pairs(a, p, 2) - 2)
                        dve.sem_inc(passed_vector, 1)
                        for e in range(2):
                            for c in range(C):
                                v_.tensor_tensor_reduce(out=att[:, p % 2, e, c, :], in0=score_bank[e][:, c * N:c * N + N], in1=mask1[:, c, :],
                                                        scale=-SCALE, scalar=FLT_MAX, op0=ALU.add, op1=ALU.min,
                                                        accum_out=nmax1[:, p, c, e:e + 1]).then_inc(masked, 1)
                    elif kind == "cos":
                        dve.wait_ge(gram_full, pairs(a, p) + 1)
                        for e in range(2):
                            for c in range(C):
                                dve.wait_ge(exp1_done, pairs(a, p, 4) + 2 * e + c + 1)
                                e_sl = att[:, p % 2, e, c, :]
                                v_.scalar_tensor_tensor(e_sl, gram_bank[e][:, c * N:c * N + N], COS_THRESHOLD, e_sl, ALU.is_gt, ALU.mult,
                                                        accum_out=usum1[:, p, c, e:e + 1]).then_inc(gated, 1)
                    elif kind == "factor":
                        dve.wait_ge(gated, pairs(a, p, 4) + 4)
                        v_.tensor_tensor(den1[:, :, :], esum1[:, p, :, :], usum1[:, p, :, :], ALU.add).then_inc(fac_steps, 1)
                        dve.wait_ge(fac_steps, pairs(a, p, 3) + 1)
                        v_.reciprocal(rec1[:, :, :], den1[:, :, :]).then_inc(fac_steps, 1)
                        dve.wait_ge(fac_steps, pairs(a, p, 3) + 2)
                        dve.wait_ge(keep_ready, a + 1)
                        v_.tensor_tensor(fac1[:, :, :], rec1[:, :, :], keep[:, :, :], ALU.mult).then_inc(fac_steps, 1)
                    elif kind == "back":
                        dve.wait_ge(fac_steps, pairs(a, p, 3) + 3)
                        dve.wait_ge(o_full, pairs(a, p) + 1)
                        dve.wait_ge(res_added, pairs(a, p))
                        v_.scalar_tensor_tensor(rel[:, :, :].rearrange("p c (e d) -> p (c e) d", d=DH),
                                                t_bank[1][:, 0:N].rearrange("p (x d) -> p x d", d=DH), 0.0,
                                                fac1[:, :, :].rearrange("p c (e o) -> p (c e) o", o=1).to_broadcast([128, 2 * C, DH]),
                                                ALU.max, ALU.mult).then_inc(rel_done, 1)
                    elif kind[:2] == "ht":
                        t = 2 * "ab".index(kind[3])
                        v_.scalar_tensor_tensor(flat(hT[:, 1, t:t + 2, :]), full[:, :], 0.0, flat(hT[:, 0, t:t + 2, :]).bitcast(F32),
                                                ALU.max, ALU.subtract).then_inc(product_done, 1)
                    elif kind[:2] == "qk":
                        w, t = int(kind[2]) % 2, int(kind[2]) // 2
                        v_.tensor_tensor(qkm[:, 1, 2 * w + t, :], full[:, 0:N], qkm[:, 0, 2 * w + t, :].bitcast(F32), ALU.subtract).then_inc(product_done, 1)
                    elif kind == "v0":
                        v_.tensor_copy(flat(v0[:, :, :]), full[:, :]).then_inc(product_done, 1)
                    elif kind in ("s0", "s1", "s2", "s3"):
                        hd = int(kind[1])
                        for c in range(C):
                            last = v_.tensor_tensor_reduce(out=prob0[:, hd, c, :], in0=full[:, c * N:c * N + N], in1=mask0[:, c, :],
                                                           scale=-SCALE, scalar=FLT_MAX, op0=ALU.add, op1=ALU.min,
                                                           accum_out=nmax0[:, hd, c:c + 1])
                        last.then_inc(product_done, 1)
                    elif kind[:3] == "sum":
                        hd = int(kind[3])
                        dve.wait_ge(exp0_done, H0 * n + hd + 1)
                        v_.reciprocal(rsum0[:, hd, :], esum0[:, hd, :]).then_inc(rsum0_done, 1)
                    elif kind == "av":
                        v_.tensor_tensor(flat(oT0[:, 1, :, :]), full[:, :], flat(oT0[:, 0, :, :]).bitcast(F32), ALU.subtract).then_inc(product_done, 1)
                    elif kind in ("wo0", "wo1"):
                        c = int(kind[2])
                        dve.wait_ge(mid_ready, 2 * n + c + 1)
                        v_.tensor_tensor(x_mid[:, c, :], full[:, :], x_mid[:, c, :], ALU.add).then_inc(product_done, 1)
                        dve.wait_ge(product_done, out_of_psum(n, kind))
                        row_stats(x_mid, c)
                        if c == 1:
                            mean_var(2 * n + 1)
                    elif kind in ("m0", "m1", "m2", "m3"):
                        t = int(kind[1])
                        v_.tensor_scalar(m32[:, t, :], full[:, 0:N], bias_m[:, t:t + 1], None, ALU.add)
                        v_.scalar_tensor_tensor(qkm[:, 1, t, :], full[:, 0:N], bias_m[:, t:t + 1], qkm[:, 0, t, :].bitcast(F32),
                                                ALU.add, ALU.subtract).then_inc(product_done, 1)
                    elif kind == "norm1":
                        normalise(2 * n + 1, x_mid)
                    elif kind == "norm0":
                        normalise(2 * n + 2, x_in)
                    elif kind == "stats0":
                        dve.wait_ge(x_loaded, 16 * n + 32)
                        row_stats(x_in, 0)
                        row_stats(x_in, 1)
                        mean_var(2 * n + 2)
                    elif kind in ("vv0", "vv1"):
                        if a is None:
                            dve.wait_ge(fold_done, KT + 1)
                        v_.tensor_tensor(v1[:, int(kind[2]), :], full[:, :], bias_v[:, :], ALU.add).then_inc(product_done, 1)
                    elif kind[0] in "qk" and kind[1].isdigit():
                        t = int(kind[1])
                        dst, bias = {"q": (q1, bias_q), "k": (k1, bias_k)}[kind[0]]
                        v_.scalar_tensor_tensor(dst[:, 1, t, :], full[:, 0:N], bias[:, t:t + 1], dst[:, 0, t, :].bitcast(F32),
                                                ALU.add, ALU.subtract).then_inc(product_done, 1)
                    elif kind == "ss":
                        v_.tensor_scalar(ssq[:, :], full[:, 0:C * H1], COS_EPS * COS_EPS, None, ALU.max).then_inc(product_done, 1)
                    elif kind == "rt":
                        v_.tensor_copy(rnT[0:H1, :], full[0:H1, 0:N]).then_inc(rt_high, 1)
                        dve.wait_ge(rt_high, n + 1)
                        v_.tensor_tensor(rnT[32:32 + H1, :], full[0:H1, 0:N], rnT[0:H1, :].bitcast(F32), ALU.subtract).then_inc(product_done, 1)
                    elif kind in ("bc0", "bc1"):
                        t = 2 * int(kind[2])
                        v_.tensor_tensor(flat(m32[:, t:t + 2, :]), full[:, :], flat(m32[:, t:t + 2, :]), ALU.mult).then_inc(product_done, 1)

            rounds(dve, body)

        @block.tensor
        def _(pe):
            t_ = nc.tensor
            pe.wait_ge(made, 9)
            pe.sem_inc(score_full, PAIRS1)
            pe.sem_inc(gram_full, PAIRS1)
            pe.sem_inc(t_full, 2 * PAIRS1)
            pe.sem_inc(uv_full, PAIRS1)
            pe.sem_inc(o_full, PAIRS1)

            def fold(kt):
                if kt == 0:
                    pe.wait_ge(pick_made, 3)
                if kt == KT:
                    pe.wait_ge(fold_done, KT)
                for half in range(2):
                    part = slice(64 * half, 64 * half + 64)
                    for i in range(4):
                        hd = 4 * half + i
                        left = gcn_rows[part, i, kt * 128:kt * 128 + 128] if kt < KT else gcn_bb[part, i, :]
                        last = t_.matmul(bank[kt % KT][:, hd * DH:hd * DH + DH], left, gcn_w[part, :], start=True, stop=True)
                    if half == 0:
                        last.then_inc(fold_half, 1)
                        pe.wait_ge(fold_half, kt + 1)
                last.then_inc(fold_full, 1)

            def transposes(dst, src_of):
                for outer in range(2):
                    for c in range(C):
                        b = 2 * outer + c
                        last = t_.transpose(dst[:, b * 128:b * 128 + 128], src_of(outer, c), ident[:, :])
                return last

            def project(dst, w, t, rhs, chunks=range(KT)):
                for k in chunks:
                    for i, (ws, rs) in enumerate(PASSES):
                        last = t_.matmul(dst, w(ws, k)[:, t * 128:t * 128 + 128], rhs[:, rs, k, :],
                                         start=(k == 0 and i == 0), stop=(k == KT - 1 and i == 2))
                return last

            def project_rows(dst, lhs, chunks, c, w):
                for k in range(chunks):
                    for i, (ls, ws) in enumerate(PASSES):
                        last = t_.matmul(dst, lhs[:, ls, k, c * 128:c * 128 + 128], w(ws, k),
                                         start=(k == 0 and i == 0), stop=(k == chunks - 1 and i == 2))
                return last

            def head_products(banks, left, right):
                last = [None, None]
                for c in range(C):
                    for i, (ls, rs) in enumerate(PASSES):
                        for e in range(2):
                            r = slice(64 * e, 64 * e + 64)
                            last[e] = t_.matmul(banks[e][:, c * N:c * N + N], left[r, ls, c * 128:c * 128 + 128], right[r, rs, :],
                                                start=(i == 0), stop=(i == 2))
                return last

            def values(dst, v, hd0, rhs):
                for jc in range(C):
                    for e in range(2):
                        last = t_.matmul(dst[64 * e:64 * e + 64, :], v[:, jc, (hd0 + e) * DH:(hd0 + e + 1) * DH], rhs(e, jc),
                                         start=(jc == 0), stop=(jc == C - 1))
                return last

            def body(a, n, more):
                for s in steps(a, n, more):
                    kind, p = s if isinstance(s, tuple) else (s, None)
                    if a is None and kind in FOLD_AT:
                        fold(FOLD_AT[kind])
                    if a is None and kind in ("qk0", "wo0", "m0", "q0", "k0", "vv0"):
                        if kind == "vv0":
                            pe.wait_ge(fold_done, KT + 1)
                        else:
                            pe.wait_ge(stage_lo, {"qk0": 3, "wo0": 4, "m0": 6, "q0": 8, "k0": 10}[kind])
                    if kind in PRODUCTS:
                        full = bank[bank_of[kind]]
                    if kind == "score":
                        pe.wait_ge(product_done, out_of_psum(a, f"k{p}"))
                        pe.wait_ge(masked, pairs(a, p, 4))
                        head_products(score_bank, q1[:, :, p, :], k1[:, :, p, :])[1].then_inc(score_full, 1)
                    elif kind == "cos":
                        pe.wait_ge(nlow_done, 2 * a + 2 + p // 2 + 1)
                        if p == 0:
                            pe.wait_ge(product_done, out_of_psum(a, "bc1"))
                        pe.wait_ge(gated, pairs(a, p, 4))
                        head_products(gram_bank, nrm[:, :, p, :], nrm[:, :, p, :])[1].then_inc(gram_full, 1)
                    elif kind == "turn":
                        for e in range(2):
                            pe.wait_ge(gated, pairs(a, p, 4) + 2 * e + 2)
                            if p == 0 and n is not None:
                                pe.wait_ge(product_done, out_of_psum(n, ("s0", "s1")[e]))
                            if e == 0:
                                pe.wait_ge(oT1_ready, pairs(a, p))
                            else:
                                pe.wait_ge(rel_done, pairs(a, p))
                            transposes(t_bank[e], lambda jc, c: att[:, p % 2, e, c, jc * 128:jc * 128 + 128]).then_inc(t_full, 1)
                    elif kind == "value":
                        pe.wait_ge(uT_ready, pairs(a, p, 2) + 2)
                        if p == 0:
                            pe.wait_ge(product_done, out_of_psum(a, "vv1"))
                        values(t_bank[0][:, 0:N], v1, 2 * p, lambda e, jc: uT[:, e, jc * N:jc * N + N]).then_inc(uv_full, 1)
                    elif kind == "back":
                        pe.wait_ge(oT1_ready, pairs(a, p) + 1)
                        for c in range(C):
                            last = t_.transpose(t_bank[1][:, c * 128:c * 128 + 128], oT1[:, c * 128:c * 128 + 128], ident[:, :])
                        last.then_inc(o_full, 1)
                    elif kind[:2] == "ht":
                        t = 2 * "ab".index(kind[3])
                        if kind[2] == "0":
                            pe.wait_ge(h_ready, 4 * n + 2)
                            if a is not None:
                                pe.wait_ge(rel_done, pairs(a, 0))
                        else:
                            pe.wait_ge(h_ready, 4 * n + 4)
                            pe.wait_ge(product_done, room(n, kind))
                        transposes(full, lambda k, c: h[:, c, (t + k) * 128:(t + k + 1) * 128]).then_inc(product_full, 1)
                    elif kind[:2] == "qk":
                        w, t = int(kind[2]) % 2, int(kind[2]) // 2
                        pe.wait_ge(product_done, room(n, kind))
                        for chunks in (range(2), range(2, 4)):
                            pe.wait_ge(product_done, out_of_psum(n, "ht0a" if chunks[0] == 0 else "ht0b"))
                            last = project(full[:, 0:N], lambda s2, k: w_qkv[:, s2, w, k, :], t, hT, chunks)
                        last.then_inc(product_full, 1)
                    elif kind == "v0":
                        pe.wait_ge(product_done, out_of_psum(n, "ht0b"))
                        pe.wait_ge(product_done, room(n, kind))
                        for c in range(C):
                            last = project_rows(full[:, c * INNER:c * INNER + INNER], hT, KT, c, lambda s2, k: w_qkv[:, s2, 2, k, :])
                        last.then_inc(product_full, 1)
                    elif kind in ("s0", "s2"):
                        t = int(kind[1]) // 2
                        pe.wait_ge(product_done, out_of_psum(n, f"qk{2 * t + 1}"))
                        if kind == "s2":
                            pe.wait_ge(product_done, room(n, "s3"))
                        pair_banks = [full, bank[bank_of[f"s{2 * t + 1}"]]]
                        for last in head_products(pair_banks, qkm[:, :, t, :], qkm[:, :, 2 + t, :]):
                            last.then_inc(product_full, 1)
                    elif kind[:2] == "pt":
                        hd = int(kind[2])
                        pe.wait_ge(prob0_done, H0 * n + hd + 1)
                        if hd < 2:
                            pe.wait_ge(product_done, room(n, kind))
                        else:
                            pe.wait_ge(pT_ready, H0 * n + hd - 1)
                        transposes(full, lambda jc, c: prob0[:, hd, c, jc * 128:jc * 128 + 128]).then_inc(product_full, 1)
                    elif kind == "av":
                        pe.wait_ge(pT_ready, H0 * n + H0)
                        for t in range(PAIRS0):
                            last = values(full[:, t * N:t * N + N], v0, 2 * t, lambda e, jc: ptm[:, 2 * t + e, jc * N:jc * N + N])
                        last.then_inc(product_full, 1)
                    elif kind in ("wo0", "wo1"):
                        pe.wait_ge(product_done, out_of_psum(n, "av"))
                        project_rows(full[:, :], oT0, PAIRS0, int(kind[2]), lambda s2, k: w_o[:, s2, k, :]).then_inc(product_full, 1)
                    elif kind in ("m0", "m1", "m2", "m3"):
                        pe.wait_ge(product_done, room(n, kind))
                        for chunks in (range(2), range(2, 4)):
                            pe.wait_ge(product_done, out_of_psum(n, "ht1a" if chunks[0] == 0 else "ht1b"))
                            last = project(full[:, 0:N], lambda s2, k: w_map[:, s2, k, :], int(kind[1]), hT, chunks)
                        last.then_inc(product_full, 1)
                    elif kind in ("vv0", "vv1"):
                        pe.wait_ge(product_done, out_of_psum(n, "ht1b"))
                        pe.wait_ge(product_done, room(n, kind))
                        project_rows(full[:, :], hT, KT, int(kind[2]), lambda s2, k: w_v[:, s2, k, :]).then_inc(product_full, 1)
                    elif kind[0] in "qk" and kind[1].isdigit():
                        pe.wait_ge(product_done, out_of_psum(n, "m3"))
                        pe.wait_ge(product_done, room(n, kind))
                        w = {"q": w_q, "k": w_k}[kind[0]]
                        project(full[:, 0:N], lambda s2, k: w[:, s2, k, :], int(kind[1]), qkm).then_inc(product_full, 1)
                    elif kind == "ss":
                        pe.wait_ge(msq_done, KT * n + KT)
                        if a is not None:
                            pe.wait_ge(masked, pairs(a, PAIRS1, 4))
                        for t in range(KT):
                            for c in range(C):
                                last = t_.matmul(full[:, c * H1 + 2 * t:c * H1 + 2 * t + 2], msq[:, t, c * 128:c * 128 + 128], half_of[:, :], start=True, stop=True)
                        last.then_inc(product_full, 1)
                    elif kind == "rt":
                        pe.wait_ge(rn_done, n + 1)
                        for c in range(C):
                            last = t_.transpose(full[0:H1, c * 128:c * 128 + 128], rn[:, c * H1:c * H1 + H1], ident[:, :])
                        last.then_inc(product_full, 1)
                    elif kind in ("bc0", "bc1"):
                        pe.wait_ge(product_done, out_of_psum(n, "rt"))
                        if a is not None:
                            pe.wait_ge(gated, pairs(a, PAIRS1, 4))
                        for t in range(2):
                            last = t_.matmul(full[:, t * N:t * N + N], pick[:, 2 * int(kind[2]) + t, :], rnT[:, :], start=True, stop=True)
                        last.then_inc(product_full, 1)

            rounds(pe, body)


def build(nc, args):
    gnn_two_layers(nc, *args)


def kernel(x, adj, L0_gnn_Wq, L0_gnn_Wk, L0_gnn_Wv, L0_gnn_Wo, L0_gnn_bo, L1_gnn_map_w, L1_gnn_map_b, L1_gnn_q_w,
           L1_gnn_q_b, L1_gnn_k_w, L1_gnn_k_b, L1_gnn_gcn_map_w, L1_gnn_gcn_map_b, L1_gnn_gcn_W):
    import concourse.bacc as bacc
    from concourse.bass_utils import run_bass_kernel_spmd

    def rows(a):
        return np.ascontiguousarray(a)

    arrays = {
        "x": rows(x), "adj": rows(adj),
        "wq": rows(L0_gnn_Wq), "wk": rows(L0_gnn_Wk), "wv": rows(L0_gnn_Wv), "wo": rows(L0_gnn_Wo), "bo": rows(L0_gnn_bo),
        "map_t": rows(np.asarray(L1_gnn_map_w).T), "map_b": rows(L1_gnn_map_b),
        "q_t": rows(np.asarray(L1_gnn_q_w).T), "q_b": rows(L1_gnn_q_b),
        "k_t": rows(np.asarray(L1_gnn_k_w).T), "k_b": rows(L1_gnn_k_b),
        "gcn_map": rows(L1_gnn_gcn_map_w), "gcn_map_b": rows(L1_gnn_gcn_map_b),
        "gcn_t": rows(np.asarray(L1_gnn_gcn_W).T),
    }
    nc = bacc.Bacc("TRN2", target_bir_lowering=False, num_devices=1)
    args = [nc.dram_tensor(n, a.shape, mybir.dt.from_np(a.dtype), kind="ExternalInput").ap() for n, a in arrays.items()]
    args.append(nc.dram_tensor("out", arrays["x"].shape, F32, kind="ExternalOutput").ap())
    build(nc, args)
    r = run_bass_kernel_spmd(nc, [arrays], core_ids=[0])
    return r.results[0]["out"]
```
